# Optimizing a Trainium2 kernel written in Bass

```python
import numpy as np
import jax
import jax.numpy as jnp

def _softmax(x, axis=-1):
    return jax.nn.softmax(x, axis=axis)

def _gelu(x):
    return jax.nn.gelu(x, approximate=True)

def _silu(x):
    return jax.nn.silu(x)

def _sigmoid(x):
    return jax.nn.sigmoid(x)

def _layernorm(x, axis=-1, eps=1e-05):
    m = jnp.mean(x, axis=axis, keepdims=True)
    v = jnp.var(x, axis=axis, keepdims=True)
    return (x - m) / jnp.sqrt(v + eps)

def _scatter_add(tgt, idx, src, axis=0):
    return tgt.at[idx].add(src)

def _segment_sum(src, seg, n):
    return jax.ops.segment_sum(src, seg, n)
kernel_name = 'mk_dlrm_tower_d1_rec_r8_5143cf'

def setup_inputs(seed: int=0):
    np.random.seed(seed)
    _w = jnp.asarray

    def _rec_inputs():
        import jax
        import jax.numpy as jnp
        _tk = jax.random.key(seed)
        dense_ctx = jax.random.normal(jax.random.fold_in(_tk, 190), (2048, 16), jnp.float32)
        ids = jnp.stack([jax.random.randint(jax.random.fold_in(_tk, 200 + f), (2048,), 0, v, jnp.int32) for f, v in enumerate([12500, 125000, 1250, 1250, 125000, 12500, 1000, 12500, 1000, 1250, 12500, 125000, 1000, 12500, 12500, 1250, 1250, 1000, 12500, 12500, 125000, 1000, 1000, 1250, 1000, 1250])], axis=1)
        tbl_0 = 0.05 * jax.random.normal(jax.random.fold_in(_tk, 500 + 0), (12500, 32), jnp.float32)
        tbl_1 = 0.05 * jax.random.normal(jax.random.fold_in(_tk, 500 + 1), (125000, 32), jnp.float32)
        tbl_2 = 0.05 * jax.random.normal(jax.random.fold_in(_tk, 500 + 2), (1250, 32), jnp.float32)
        tbl_3 = 0.05 * jax.random.normal(jax.random.fold_in(_tk, 500 + 3), (1250, 32), jnp.float32)
        tbl_4 = 0.05 * jax.random.normal(jax.random.fold_in(_tk, 500 + 4), (125000, 32), jnp.float32)
        tbl_5 = 0.05 * jax.random.normal(jax.random.fold_in(_tk, 500 + 5), (12500, 32), jnp.float32)
        tbl_6 = 0.05 * jax.random.normal(jax.random.fold_in(_tk, 500 + 6), (1000, 32), jnp.float32)
        tbl_7 = 0.05 * jax.random.normal(jax.random.fold_in(_tk, 500 + 7), (12500, 32), jnp.float32)
        tbl_8 = 0.05 * jax.random.normal(jax.random.fold_in(_tk, 500 + 8), (1000, 32), jnp.float32)
        tbl_9 = 0.05 * jax.random.normal(jax.random.fold_in(_tk, 500 + 9), (1250, 32), jnp.float32)
        tbl_10 = 0.05 * jax.random.normal(jax.random.fold_in(_tk, 500 + 10), (12500, 32), jnp.float32)
        tbl_11 = 0.05 * jax.random.normal(jax.random.fold_in(_tk, 500 + 11), (125000, 32), jnp.float32)
        tbl_12 = 0.05 * jax.random.normal(jax.random.fold_in(_tk, 500 + 12), (1000, 32), jnp.float32)
        tbl_13 = 0.05 * jax.random.normal(jax.random.fold_in(_tk, 500 + 13), (12500, 32), jnp.float32)
        tbl_14 = 0.05 * jax.random.normal(jax.random.fold_in(_tk, 500 + 14), (12500, 32), jnp.float32)
        tbl_15 = 0.05 * jax.random.normal(jax.random.fold_in(_tk, 500 + 15), (1250, 32), jnp.float32)
        tbl_16 = 0.05 * jax.random.normal(jax.random.fold_in(_tk, 500 + 16), (1250, 32), jnp.float32)
        tbl_17 = 0.05 * jax.random.normal(jax.random.fold_in(_tk, 500 + 17), (1000, 32), jnp.float32)
        tbl_18 = 0.05 * jax.random.normal(jax.random.fold_in(_tk, 500 + 18), (12500, 32), jnp.float32)
        tbl_19 = 0.05 * jax.random.normal(jax.random.fold_in(_tk, 500 + 19), (12500, 32), jnp.float32)
        tbl_20 = 0.05 * jax.random.normal(jax.random.fold_in(_tk, 500 + 20), (125000, 32), jnp.float32)
        tbl_21 = 0.05 * jax.random.normal(jax.random.fold_in(_tk, 500 + 21), (1000, 32), jnp.float32)
        tbl_22 = 0.05 * jax.random.normal(jax.random.fold_in(_tk, 500 + 22), (1000, 32), jnp.float32)
        tbl_23 = 0.05 * jax.random.normal(jax.random.fold_in(_tk, 500 + 23), (1250, 32), jnp.float32)
        tbl_24 = 0.05 * jax.random.normal(jax.random.fold_in(_tk, 500 + 24), (1000, 32), jnp.float32)
        tbl_25 = 0.05 * jax.random.normal(jax.random.fold_in(_tk, 500 + 25), (1250, 32), jnp.float32)
        _rk = jax.random.fold_in(_tk, 7)
        W_top1 = 0.0606339 * jax.random.normal(jax.random.fold_in(_tk, 801), (272, 512), jnp.float32)
        W_top2 = 0.0441942 * jax.random.normal(jax.random.fold_in(_tk, 802), (512, 256), jnp.float32)
        W_top3 = 0.0625 * jax.random.normal(jax.random.fold_in(_tk, 803), (256, 1), jnp.float32)
        b_top1 = jnp.zeros((512,), jnp.float32)
        b_top2 = jnp.zeros((256,), jnp.float32)
        return (dense_ctx, ids, tbl_0, tbl_1, tbl_2, tbl_3, tbl_4, tbl_5, tbl_6, tbl_7, tbl_8, tbl_9, tbl_10, tbl_11, tbl_12, tbl_13, tbl_14, tbl_15, tbl_16, tbl_17, tbl_18, tbl_19, tbl_20, tbl_21, tbl_22, tbl_23, tbl_24, tbl_25, W_top1, b_top1, W_top2, b_top2, W_top3)
    dense_ctx, ids, tbl_0, tbl_1, tbl_2, tbl_3, tbl_4, tbl_5, tbl_6, tbl_7, tbl_8, tbl_9, tbl_10, tbl_11, tbl_12, tbl_13, tbl_14, tbl_15, tbl_16, tbl_17, tbl_18, tbl_19, tbl_20, tbl_21, tbl_22, tbl_23, tbl_24, tbl_25, W_top1, b_top1, W_top2, b_top2, W_top3 = _rec_inputs()

    def _L0_rec_setup():
        import jax, jax.numpy as jnp
        import numpy as np
        M_FIELDS = 26
        H1 = 128
        H2 = 128
        BATCH = 256
        EMB_K = 32

        def _cin_layer(x_prev, x0, W, b):
            return jnp.einsum('bik,bjk,hij->bhk', x_prev, x0, W) + b[None, :, None]
        key = jax.random.key(seed)
        k0, k1, k2, k3, k4 = jax.random.split(key, 5)
        inputs = jax.random.normal(k0, (BATCH, M_FIELDS, EMB_K), dtype=jnp.float32)
        W1 = jax.random.normal(k1, (H1, M_FIELDS, M_FIELDS), dtype=jnp.float32) * 0.05
        b1 = jax.random.normal(k2, (H1,), dtype=jnp.float32) * 0.05
        W2 = jax.random.normal(k3, (H2, H1, M_FIELDS), dtype=jnp.float32) * 0.05
        b2 = jax.random.normal(k4, (H2,), dtype=jnp.float32) * 0.05
        return {'inputs': inputs, 'W1': W1, 'b1': b1, 'W2': W2, 'b2': b2}
    _L0_rec_all = _L0_rec_setup()
    _L0_rec_in = {k: v for k, v in _L0_rec_all.items() if k in ('W1', 'b1', 'W2', 'b2')}
    del _L0_rec_all
    return {'dense_ctx': dense_ctx, 'ids': ids, 'tbl_0': tbl_0, 'tbl_1': tbl_1, 'tbl_2': tbl_2, 'tbl_3': tbl_3, 'tbl_4': tbl_4, 'tbl_5': tbl_5, 'tbl_6': tbl_6, 'tbl_7': tbl_7, 'tbl_8': tbl_8, 'tbl_9': tbl_9, 'tbl_10': tbl_10, 'tbl_11': tbl_11, 'tbl_12': tbl_12, 'tbl_13': tbl_13, 'tbl_14': tbl_14, 'tbl_15': tbl_15, 'tbl_16': tbl_16, 'tbl_17': tbl_17, 'tbl_18': tbl_18, 'tbl_19': tbl_19, 'tbl_20': tbl_20, 'tbl_21': tbl_21, 'tbl_22': tbl_22, 'tbl_23': tbl_23, 'tbl_24': tbl_24, 'tbl_25': tbl_25, 'W_top1': W_top1, 'b_top1': b_top1, 'W_top2': W_top2, 'b_top2': b_top2, 'W_top3': W_top3, 'L0_rec_W1': _L0_rec_in['W1'], 'L0_rec_b1': _L0_rec_in['b1'], 'L0_rec_W2': _L0_rec_in['W2'], 'L0_rec_b2': _L0_rec_in['b2']}

def reference(dense_ctx, ids, tbl_0, tbl_1, tbl_2, tbl_3, tbl_4, tbl_5, tbl_6, tbl_7, tbl_8, tbl_9, tbl_10, tbl_11, tbl_12, tbl_13, tbl_14, tbl_15, tbl_16, tbl_17, tbl_18, tbl_19, tbl_20, tbl_21, tbl_22, tbl_23, tbl_24, tbl_25, W_top1, b_top1, W_top2, b_top2, W_top3, L0_rec_W1, L0_rec_b1, L0_rec_W2, L0_rec_b2):
    import jax
    import jax.numpy as jnp

    def _L0_rec_ref(inputs, W1, b1, W2, b2):
        import jax, jax.numpy as jnp
        import numpy as np
        M_FIELDS = 26
        H1 = 128
        H2 = 128
        BATCH = 256
        EMB_K = 32

        def _cin_layer(x_prev, x0, W, b):
            return jnp.einsum('bik,bjk,hij->bhk', x_prev, x0, W) + b[None, :, None]
        x1 = _cin_layer(inputs, inputs, W1, b1)
        x2 = _cin_layer(x1, inputs, W2, b2)
        res = jnp.concatenate([x1, x2], axis=1)
        return jnp.sum(res, axis=-1)
    e = jnp.stack([tbl_0[ids[:, 0]], tbl_1[ids[:, 1]], tbl_2[ids[:, 2]], tbl_3[ids[:, 3]], tbl_4[ids[:, 4]], tbl_5[ids[:, 5]], tbl_6[ids[:, 6]], tbl_7[ids[:, 7]], tbl_8[ids[:, 8]], tbl_9[ids[:, 9]], tbl_10[ids[:, 10]], tbl_11[ids[:, 11]], tbl_12[ids[:, 12]], tbl_13[ids[:, 13]], tbl_14[ids[:, 14]], tbl_15[ids[:, 15]], tbl_16[ids[:, 16]], tbl_17[ids[:, 17]], tbl_18[ids[:, 18]], tbl_19[ids[:, 19]], tbl_20[ids[:, 20]], tbl_21[ids[:, 21]], tbl_22[ids[:, 22]], tbl_23[ids[:, 23]], tbl_24[ids[:, 24]], tbl_25[ids[:, 25]]], axis=1)
    z = _L0_rec_ref(e, L0_rec_W1, L0_rec_b1, L0_rec_W2, L0_rec_b2)
    z = z.reshape(z.shape[0], -1)
    h = jnp.concatenate([z, dense_ctx], axis=1)
    h = jnp.maximum(h @ W_top1 + b_top1, 0.0)
    h = jnp.maximum(h @ W_top2 + b_top2, 0.0)
    y = h @ W_top3
    return y

_drawn_inputs = setup_inputs


def setup_inputs(seed=0):
    import zlib

    import numpy as np

    out = dict(_drawn_inputs(seed))
    spreads = {'b_top1': (0.0, 2.0), 'b_top2': (0.0, 0.8)}
    factors = {'tbl_0': 8.0,
     'tbl_1': 8.0,
     'tbl_2': 8.0,
     'tbl_3': 8.0,
     'tbl_4': 8.0,
     'tbl_5': 8.0,
     'tbl_6': 8.0,
     'tbl_7': 8.0,
     'tbl_8': 8.0,
     'tbl_9': 8.0,
     'tbl_10': 8.0,
     'tbl_11': 8.0,
     'tbl_12': 8.0,
     'tbl_13': 8.0,
     'tbl_14': 8.0,
     'tbl_15': 8.0,
     'tbl_16': 8.0,
     'tbl_17': 8.0,
     'tbl_18': 8.0,
     'tbl_19': 8.0,
     'tbl_20': 8.0,
     'tbl_21': 7.832,
     'tbl_22': 8.0,
     'tbl_23': 8.0,
     'tbl_24': 8.0,
     'tbl_25': 8.0,
     'L0_rec_W1': 8.0,
     'L0_rec_W2': 4.286,
     'dense_ctx': 6.194}
    for name, (base, spread) in spreads.items():
        noise = np.random.default_rng([zlib.crc32(name.encode()), seed]).standard_normal(out[name].shape)
        drawn = base * np.exp(spread * noise) if base else spread * noise
        out[name] = jnp.asarray(drawn.astype(out[name].dtype))
    for name, factor in factors.items():
        out[name] = (out[name] * factor).astype(out[name].dtype)
    return out
```

```python
from contextlib import ExitStack

import concourse.bass as bass
from concourse import mybir

F32 = mybir.dt.float32
I32 = mybir.dt.int32
ALU = mybir.AluOpType
ACT = mybir.ActivationFunctionType


def tri(n):
    return n * (n + 1) // 2


def build_dlrm_tower(nc, t):
    B, F = t["ids"].shape
    K = t["tbl_0"].shape[1]
    H = t["W1"].shape[0]
    DC = t["denseT"].shape[0]
    N1 = t["W_top1"].shape[1]
    N2 = t["W_top2"].shape[1]
    Q = 128 // K
    TILE = 128
    GR = TILE // Q
    HG = GR // 2
    CT = 2
    CB = CT * TILE
    CHUNKS = B // CB
    QUAD = 4
    QT = GR // QUAD
    QC = CT * QT
    QH = HG // QUAD

    FH = F // 2
    LOW = 4
    NP = F + 1
    CONST = FH
    HI = tri(FH) - tri(LOW)
    ROW_AHI = FH + 1
    ROW_ALO = ROW_AHI + HI
    ROW_BLO = ROW_ALO + tri(LOW)
    ROW_BHI = ROW_BLO + tri(LOW)
    ROWS = ROW_BHI + HI
    Y_ROWS = ROW_BHI
    X_ROWS = ROWS - ROW_ALO
    COLS = NP - LOW
    W1N = F * F + 1
    CU = -(-FH // 4)

    UY, UZ_Y, UX = 0, COLS, COLS + 1
    UZ_X, UZ_C = UX + COLS, UX + COLS + 1
    UNITS = UZ_C + CU

    def pos(f):
        return f if f < FH else f + 1

    def block(half, q):
        return (0, q, q) if half == 0 else (F - 1 - q, F - 1, F - 1 - q)

    def row(half, q):
        if half == 0:
            return ROW_ALO + tri(q) if q < LOW else ROW_AHI + tri(q) - tri(LOW)
        return ROW_BLO + tri(q) if q < LOW else ROW_BHI + tri(q) - tri(LOW)

    with ExitStack() as ctx:
        def sb(name, shape, dt=F32):
            return ctx.enter_context(nc.sbuf_tensor(name, shape, dt))

        def bank(name):
            return ctx.enter_context(nc.psum_tensor(name, [128, 512], F32))

        def sem(name):
            return ctx.enter_context(nc.semaphore(name))

        idx = sb("idx", [128, CT, F], I32)
        emb = sb("emb", [128, CT, NP, K])
        embT = sb("embT", [128, CT, NP, GR])
        P = sb("P", [128, 2, HG, ROWS])
        M = sb("M", [128, 2, HG, Q, NP])
        wz = sb("wz", [128, UNITS, H])
        w1 = sb("w1", [128, F, F])
        w1s = sb("w1s", [128, W1N])
        w2t = sb("w2t", [128, F, H])
        b12 = sb("b12", [128, 2])
        ident = sb("ident", [128, 128])
        wt1 = sb("wt1", [128, 3, N1])
        wt2 = sb("wt2", [128, N1 // 128, N2])
        wt3 = sb("wt3", [128, N2 // 128])
        bt = sb("bt", [128, N1 // 128 + N2 // 128])
        dense = sb("dense", [DC, B])
        yrow = sb("yrow", [1, B])
        Dbuf = sb("Dbuf", [128, F * W1N])
        D = Dbuf[:, :].rearrange("h (x c) -> h x c", x=F)
        D4 = D[:, :, 0:F * F].rearrange("h x (y z) -> h x y z", y=F)
        TN = COLS * CB
        TY = Dbuf[:, 0:TN].rearrange("p (j b) -> p j b", j=COLS)
        TX = Dbuf[:, TN:2 * TN].rearrange("p (j b) -> p j b", j=COLS)
        o = 2 * TN
        TC = Dbuf[:, o:o + CU * CB].rearrange("p (u b) -> p u b", u=CU)
        o += CU * CB
        zs = Dbuf[:, o:o + 2 * CB].rearrange("p (z b) -> p z b", z=2)
        o += 2 * CB
        h1 = Dbuf[:, o:o + N1 // 128 * CB].rearrange("p (m b) -> p m b", b=CB)
        o += N1 // 128 * CB
        h2 = Dbuf[:, o:o + N2 // 128 * CB].rearrange("p (m b) -> p m b", b=CB)
        assert o + N2 // 128 * CB <= F * W1N
        stY = sb("stY", [128, COLS + 1, Y_ROWS])
        XN = (COLS + 1) * X_ROWS
        w2flat = w2t[:, :, :].rearrange("i x h -> i (x h)")
        stX = w2flat[:, 0:XN].rearrange("h (u r) -> h u r", u=COLS + 1)
        stC = w2flat[:, XN:XN + CU * 128].rearrange("h (u r) -> h u r", u=CU)
        assert XN + CU * 128 <= F * H

        psT = [bank(f"psT{i}") for i in range(4)]
        psZ = bank("psZ")
        psH = [bank(f"psH{i}") for i in range(2)]
        psO = bank("psO")

        w_in = sem("w_in")
        mlp_in = sem("mlp_in")
        idx_in = [sem(f"idx_in{i}") for i in range(CT)]
        gathered = [sem(f"gathered{i}") for i in range(CT)]
        slot_free = sem("slot_free")
        ones_set = sem("ones_set")
        ident_in = sem("ident_in")
        transposed = sem("transposed")
        prepared = sem("prepared")
        moments = sem("moments")
        kept = sem("kept")
        crossed = sem("crossed")
        z_done = sem("z_done")
        z_kept = sem("z_kept")
        h1_done = sem("h1_done")
        h1_kept = sem("h1_kept")
        h2_done = sem("h2_done")
        h2_kept = sem("h2_kept")
        y_done = sem("y_done")
        y_kept = sem("y_kept")
        stored = sem("stored")
        w1_sym = sem("w1_sym")
        d_done = sem("d_done")
        d_kept = sem("d_kept")
        st_step = sem("st_step")
        wz_done = sem("wz_done")
        wz_kept = sem("wz_kept")
        cross_zero = sem("cross_zero")

        staged = {}

        block_ = ctx.enter_context(nc.Block())

        DH = -(-W1N // 2)
        wz_sets = []
        for stage, unit, n, rows in ((stY, UY, COLS + 1, Y_ROWS), (stX, UX, COLS + 1, X_ROWS), (stC, UZ_C, CU, 128)):
            wz_sets += [(stage, a, unit + a, min(4, n - a), rows) for a in range(0, n, 4)]
        Y_SETS = -(-(COLS + 1) // 4)

        @block_.sync
        def _(sp):
            for i in range(CT):
                sp.dma_start(idx[:, i, :], t["ids"][i * TILE:(i + 1) * TILE, :]).then_inc(idx_in[i], 16)
            sp.dma_start(w1[:, :, :], t["W1"]).then_inc(w_in, 16)
            sp.dma_start(b12[:, :], t["b12"]).then_inc(w_in, 16)
            sp.dma_start(w2t[:, :, :], t["W2t"]).then_inc(w_in, 16)
            sp.dma_start(ident[:, :], t["ident"]).then_inc(ident_in, 16)
            sp.dma_start(wt1[:, 0:2, :], t["W_top1"][0:2 * H, :].rearrange("(c p) n -> p c n", p=H)).then_inc(mlp_in, 16)
            sp.dma_start(wt1[0:DC, 2, :], t["W_top1"][2 * H:2 * H + DC, :]).then_inc(mlp_in, 16)
            sp.dma_start(wt2[:, :, :], t["W_top2"].rearrange("(c p) n -> p c n", p=128)).then_inc(mlp_in, 16)
            sp.dma_start(wt3[:, :], t["W_top3p"]).then_inc(mlp_in, 16)
            sp.dma_start(bt[:, :], t["b_top"]).then_inc(mlp_in, 16)
            sp.dma_start(dense[:, :], t["denseT"]).then_inc(mlp_in, 16)
            with sp.Fori(0, CHUNKS - 1) as c:
                for i in range(CT):
                    sp.wait_ge(gathered[i], c * (16 * F) + 16 * F)
                    sp.dma_start(idx[:, i, :],
                                 t["ids"][bass.ds(c * CB + (CB + i * TILE), TILE), :]).then_inc(idx_in[i], 16)
            sp.wait_ge(y_kept, CHUNKS)
            sp.dma_start(t["y"], yrow[:, :]).then_inc(stored, 16)
            sp.wait_ge(stored, 16)

        @block_.gpsimd
        def _(pool):
            def gather(c, first):
                for i in range(CT):
                    if not first:
                        pool.wait_ge(idx_in[i], 16 * c + 16)
                        pool.wait_ge(transposed, CT * c - (CT - 1 - i))
                        pool.sem_inc(slot_free, 1)
                    else:
                        pool.wait_ge(idx_in[i], 16)
                    for f in range(F):
                        pool.indirect_dma_start(
                            out=emb[:, i, pos(f), :], out_offset=None, in_=t[f"tbl_{f}"],
                            in_offset=bass.IndirectOffsetOnAxis(ap=idx[:, i, f:f + 1], axis=0),
                        ).then_inc(gathered[i], 16)

            gather(0, True)
            with pool.Fori(1, CHUNKS) as c:
                gather(c, False)

        @block_.vector
        def _(dve):
            steps = [0]

            def step(ins):
                steps[0] += 1
                ins.then_inc(st_step, 1)

            def settle():
                dve.wait_ge(st_step, steps[0])

            nc.vector.memset(emb[:, :, CONST, :], 1.0).then_inc(ones_set, 1)
            step(nc.vector.memset(M[:, :, :, :, :], 0.0))
            step(nc.vector.memset(stY[:, :, :], 0.0))
            settle()

            dve.wait_ge(w_in, 48)
            ws3 = w1s[:, 0:F * F].rearrange("i (y z) -> i y z", y=F)
            step(nc.vector.tensor_tensor(ws3, w1[:, :, :], w1[:, :, :].rearrange("i y z -> i z y"), ALU.add))
            settle()
            diag = slice(0, F * F, F + 1)
            w1flat = w1[:, :, :].rearrange("i y z -> i (y z)")
            step(nc.vector.tensor_copy(w1s[:, diag], w1flat[:, diag]))
            nc.vector.tensor_copy(w1s[:, F * F:W1N], b12[:, 0:1]).then_inc(w1_sym, 1)
            settle()

            def fill(stage, r0, half, q, f0, f1, unit0, own):
                lo, hi, s = block(half, q)
                r = row(half, q) - r0
                a, b = (s + 1, f1) if half == 0 else (f0, s - 1)
                if not own:
                    a, b = f0, f1
                n = hi - lo + 1
                if own:
                    step(nc.vector.tensor_copy(stage[:, unit0 + s - f0, r:r + n], D4[:, s, s, lo:hi + 1]))
                if b >= a:
                    step(nc.vector.tensor_tensor(stage[:, unit0 + a - f0:unit0 + b + 1 - f0, r:r + n],
                                                 D4[:, a:b + 1, s, lo:hi + 1], D4[:, s, a:b + 1, lo:hi + 1], ALU.add))
                if q > 0:
                    third.append((stage, unit0, f0, (min(a, s), max(b, s)) if own else (a, b), half, s, lo, hi, r))

            def fill_third():
                settle()
                for stage, unit0, f0, (a, b), half, s, lo, hi, r in third:
                    lo2, hi2, r2 = (lo, hi - 1, r) if half == 0 else (lo + 1, hi, r + 1)
                    out = stage[:, unit0 + a - f0:unit0 + b + 1 - f0, r2:r2 + hi2 - lo2 + 1]
                    step(nc.vector.tensor_tensor(out, out, D4[:, lo2:hi2 + 1, s, a:b + 1].rearrange("h p j -> h j p"),
                                                 ALU.add))
                third.clear()

            def tile_of(c, i, first):
                dve.wait_ge(gathered[i], c * (16 * F) + 16 * F)
                if first and i == 0:
                    dve.wait_ge(ones_set, 1)
                nc.vector.transpose(embT[:, i, :, :].rearrange("p a b -> p (a b)"),
                                    emb[:, i, :, :].rearrange("p a b -> p (a b)")).then_inc(transposed, 1)
                dve.wait_ge(transposed, c * CT + i + 1)
                for hf in range(2):
                    n = i * 2 + hf
                    if not (first and n < 2):
                        dve.wait_ge(moments, QC * c + QH * (n - 1))
                    g0, g1 = hf * HG, hf * HG + HG
                    nc.vector.tensor_copy(P[:, hf, :, 0:FH + 1],
                                          embT[:, i, 0:FH + 1, g0:g1].rearrange("p f r -> p r f"))
                    for q4 in range(Q):
                        s = slice(32 * q4, 32 * q4 + 32)
                        nc.vector.tensor_copy(M[s, hf, :, q4, :],
                                              embT[s, i, :, g0:g1].rearrange("p f r -> p r f"))
                    for half in range(2):
                        for q in range(FH):
                            lo, hi, s = (pos(x) for x in block(half, q))
                            n = hi - lo + 1
                            r = row(half, q)
                            last = nc.vector.tensor_tensor(
                                P[:, hf, :, r:r + n], embT[:, i, lo:hi + 1, g0:g1].rearrange("p f r -> p r f"),
                                embT[:, i, s:s + 1, g0:g1].rearrange("p f r -> p r f").to_broadcast([128, HG, n]),
                                ALU.mult)
                    last.then_inc(prepared, 1)

            def cross(c):
                dve.wait_ge(kept, QC * c + QC)
                if isinstance(c, int):
                    dve.wait_ge(cross_zero, 1)
                for m in range(4):
                    n = len(range(m, FH, 4))
                    j = CONST + 1 - LOW + m
                    ins = nc.vector.tensor_copy(TC[32 * m:32 * m + FH + 1, 0:n, :],
                                                TY[0:FH + 1, j:j + 4 * (n - 1) + 1:4, :])
                ins.then_inc(crossed, 1)

            tile_of(0, 0, True)

            third = []
            dve.wait_ge(d_kept, 2 * F)
            uB = CONST + 1 - LOW
            for q in range(FH):
                fill(stY, 0, 0, q, FH, F - 1, uB, False)
                if q >= LOW:
                    fill(stY, 0, 0, q, LOW, FH - 1, 0, True)
                else:
                    fill(stY, 0, 1, q, FH, F - 1, uB, True)
            fill_third()
            step(nc.vector.tensor_copy(stY[:, uB:COLS, CONST], D[:, FH:F, F * F]))
            step(nc.vector.tensor_copy(stY[:, CONST - LOW, 0:FH], D[:, 0:FH, F * F]))
            step(nc.vector.tensor_copy(stY[:, CONST - LOW, CONST:CONST + 1], b12[:, 1:2]))
            step(nc.vector.tensor_copy(stY[:, COLS, CONST:CONST + 1], b12[:, 0:1]))
            for q in range(FH):
                r = row(0, q)
                step(nc.vector.tensor_copy(stY[:, COLS, r:r + q + 1], ws3[:, q, 0:q + 1]))
            settle()
            staged["Y"] = steps[0]
            step(nc.vector.memset(w2flat[:, 0:XN + CU * 128], 0.0))
            settle()
            for q in range(FH):
                fill(stX, ROW_ALO, 1, q, 0, FH - 1, 0, False)
                if q >= LOW:
                    fill(stX, ROW_ALO, 1, q, FH, F - 1 - LOW, CONST + 1, True)
                else:
                    fill(stX, ROW_ALO, 0, q, 0, FH - 1, 0, True)
            fill_third()
            for q in range(FH):
                lo, hi, s = block(1, q)
                r = row(1, q) - ROW_ALO
                step(nc.vector.tensor_copy(stX[:, COLS, r:r + q + 1], ws3[:, s, lo:hi + 1]))
            for m in range(4):
                n = len(range(m, FH, 4))
                step(nc.vector.tensor_copy(stC[:, 0:n, 32 * m:32 * m + FH],
                                           ws3[:, FH + m:FH + m + 4 * (n - 1) + 1:4, 0:FH]))
            settle()
            staged["X"] = steps[0]
            nc.vector.memset(TC[:, :, :], 0.0).then_inc(cross_zero, 1)

            tile_of(0, 1, True)
            cross(0)
            with dve.Fori(1, CHUNKS) as c:
                for i in range(CT):
                    tile_of(c, i, False)
                cross(c)

        @block_.tensor
        def _(pe):
            pe.wait_ge(w_in, 48)
            pe.wait_ge(w1_sym, 1)
            for d in range(2 * F):
                x, c0, c1 = d // 2, d % 2 * DH, min(d % 2 * DH + DH, W1N)
                if d >= 4:
                    pe.wait_ge(d_kept, d - 3)
                nc.tensor.matmul(psT[d % 4][:, 0:c1 - c0], w2t[:, x, :], w1s[:, c0:c1],
                                 start=True, stop=True).then_inc(d_done, 1)

            pe.wait_ge(ident_in, 16)
            for n, (stage, a, _, units, rows) in enumerate(wz_sets):
                pe.wait_ge(st_step, staged["Y" if n < Y_SETS else "X"])
                if n >= 2:
                    pe.wait_ge(wz_kept, n - 1)
                for k in range(units):
                    last = nc.tensor.transpose(psH[n % 2][0:rows, k * H:k * H + H], stage[:, a + k, :], ident[:, :])
                last.then_inc(wz_done, 1)

            def moments_of(c):
                for n in range(2 * CT):
                    pe.wait_ge(prepared, 2 * CT * c + n + 1)
                    for m in range(QH):
                        k = n * QH + m
                        if not (isinstance(c, int) and k < 2):
                            pe.wait_ge(kept, QC * c + k - 1)
                        for g in range(QUAD):
                            r = m * QUAD + g
                            cols = slice(g * Q * COLS, (g + 1) * Q * COLS)
                            nc.tensor.matmul(psT[k % 2][0:Y_ROWS, cols], P[:, n % 2, r, 0:Y_ROWS],
                                             M[:, n % 2, r, :, LOW:NP], start=True, stop=True)
                            last = nc.tensor.matmul(psT[2 + k % 2][0:X_ROWS, cols], P[:, n % 2, r, ROW_ALO:ROWS],
                                                    M[:, n % 2, r, :, 0:COLS], start=True, stop=True)
                        last.then_inc(moments, 1)

            z2_units = [(UY + u, Y_ROWS, TY[0:Y_ROWS, u, :]) for u in range(COLS)]
            z2_units += [(UX + u, X_ROWS, TX[0:X_ROWS, u, :]) for u in range(COLS) if u != CONST]
            z1_units = [(UZ_Y, Y_ROWS, TY[0:Y_ROWS, CONST - LOW, :]), (UZ_X, X_ROWS, TX[0:X_ROWS, CONST, :])]
            z1_units += [(UZ_C + u, 128, TC[:, u, :]) for u in range(CU)]

            def contract(out, units, part, parts):
                n0, n1 = len(units) * part // parts, len(units) * (part + 1) // parts
                for n in range(n0, n1):
                    unit, rows, rhs = units[n]
                    last = nc.tensor.matmul(out, wz[0:rows, unit, :], rhs, start=(n == 0), stop=(n == len(units) - 1))
                return last

            def z2_of(c, part):
                if part == 0:
                    pe.wait_ge(kept, QC * c + QC)
                contract(psZ[:, CB:2 * CB], z2_units, part, 2)

            def z1_of(c):
                pe.wait_ge(crossed, c + 1)
                contract(psZ[:, 0:CB], z1_units, 0, 1).then_inc(z_done, 1)

            def layer1(c):
                pe.wait_ge(z_kept, c + 1)
                if not (isinstance(c, int) and c == 0):
                    pe.wait_ge(h2_kept, N2 // 128 * c)
                for m in range(N1 // 128):
                    out = psH[m // 2][:, m % 2 * CB:m % 2 * CB + CB]
                    cols = slice(m * 128, m * 128 + 128)
                    nc.tensor.matmul(out, wt1[:, 0, cols], zs[:, 0, :], start=True, stop=False)
                    nc.tensor.matmul(out, wt1[:, 1, cols], zs[:, 1, :], start=False, stop=False)
                    nc.tensor.matmul(out, wt1[0:DC, 2, cols], dense[:, bass.ds(c * CB, CB)],
                                     start=False, stop=True).then_inc(h1_done, 1)

            def layer2(c):
                for m in range(N2 // 128):
                    for k in range(N1 // 128):
                        if m == 0:
                            pe.wait_ge(h1_kept, N1 // 128 * c + max(k + 1, 2))
                        last = nc.tensor.matmul(psH[0][:, m * CB:m * CB + CB], wt2[:, k, m * 128:m * 128 + 128],
                                                h1[:, k, :], start=(k == 0), stop=(k == N1 // 128 - 1))
                    last.then_inc(h2_done, 1)

            def layer3(c):
                pe.wait_ge(h2_kept, N2 // 128 * c + N2 // 128)
                if not (isinstance(c, int) and c == 0):
                    pe.wait_ge(y_kept, c)
                for k in range(N2 // 128):
                    last = nc.tensor.matmul(psO[0:1, 0:CB], wt3[:, k:k + 1], h2[:, k, :],
                                            start=(k == 0), stop=(k == N2 // 128 - 1))
                last.then_inc(y_done, 1)

            pe.wait_ge(d_kept, 2 * F)
            pe.wait_ge(wz_kept, len(wz_sets))
            pe.wait_ge(mlp_in, 6 * 16)
            moments_of(0)
            z2_of(0, 0)
            z2_of(0, 1)
            z1_of(0)

            def round_(c, before):
                moments_of(c)
                layer1(before)
                z2_of(c, 0)
                layer2(before)
                z2_of(c, 1)
                layer3(before)
                z1_of(c)

            round_(1, 0)
            with pe.Fori(2, CHUNKS) as c:
                round_(c, c - 1)
            layer1(CHUNKS - 1)
            layer2(CHUNKS - 1)
            layer3(CHUNKS - 1)

        @block_.scalar
        def _(act):
            for d in range(2 * F):
                x, c0, c1 = d // 2, d % 2 * DH, min(d % 2 * DH + DH, W1N)
                act.wait_ge(d_done, d + 1)
                nc.scalar.activation(D[:, x, c0:c1], psT[d % 4][:, 0:c1 - c0], ACT.Copy).then_inc(d_kept, 1)
            for n, (_, _, unit, units, rows) in enumerate(wz_sets):
                act.wait_ge(wz_done, n + 1)
                nc.scalar.activation(wz[0:rows, unit:unit + units, :],
                                     psH[n % 2][0:rows, 0:units * H].rearrange("p (u h) -> p u h", h=H),
                                     ACT.Copy).then_inc(wz_kept, 1)

            def keep_moments(c):
                for k in range(QC):
                    act.wait_ge(moments, QC * c + k + 1)
                    b = slice(k * QUAD * Q, (k + 1) * QUAD * Q)
                    for rows, out, ps in ((Y_ROWS, TY, psT[k % 2]), (X_ROWS, TX, psT[2 + k % 2])):
                        last = nc.scalar.activation(
                            out[0:rows, :, b], ps[0:rows, 0:QUAD * Q * COLS].rearrange("p (x j) -> p j x", j=COLS),
                            ACT.Copy)
                    last.then_inc(kept, 1)

            def keep_z(c):
                act.wait_ge(z_done, c + 1)
                nc.scalar.activation(zs[:, :, :], psZ[:, :].rearrange("p (z b) -> p z b", z=2),
                                     ACT.Copy).then_inc(z_kept, 1)

            def keep_mlp(c):
                for m in range(N1 // 128):
                    act.wait_ge(h1_done, N1 // 128 * c + m // 2 * 2 + 2)
                    nc.scalar.activation(h1[:, m, :], psH[m // 2][:, m % 2 * CB:m % 2 * CB + CB], ACT.Relu,
                                         bias=bt[:, m:m + 1]).then_inc(h1_kept, 1)
                act.wait_ge(h2_done, N2 // 128 * c + N2 // 128)
                for m in range(N2 // 128):
                    nc.scalar.activation(h2[:, m, :], psH[0][:, m * CB:m * CB + CB], ACT.Relu,
                                         bias=bt[:, N1 // 128 + m:N1 // 128 + m + 1]).then_inc(h2_kept, 1)
                act.wait_ge(y_done, c + 1)
                nc.scalar.activation(
                    yrow[0:1, bass.ds(c * CB, CB)].rearrange("o (t q r) -> o t r q", t=CT, q=Q),
                    psO[0:1, 0:CB].rearrange("o (t r q) -> o t r q", t=CT, q=Q), ACT.Copy).then_inc(y_kept, 1)

            act.wait_ge(mlp_in, 6 * 16)
            act.wait_ge(st_step, staged["X"])
            keep_moments(0)
            keep_z(0)
            with act.Fori(1, CHUNKS) as c:
                keep_moments(c)
                keep_mlp(c - 1)
                keep_z(c)
            keep_mlp(CHUNKS - 1)


def kernel(**inputs):
    import numpy as np
    import concourse.bacc as bacc
    from concourse.bass_utils import run_bass_kernel_spmd

    B, F = inputs["ids"].shape
    K = inputs["tbl_0"].shape[1]
    Q, GR = 128 // K, 128 // (128 // K)
    a = {f"tbl_{f}": inputs[f"tbl_{f}"] for f in range(F)}
    a["ids"] = inputs["ids"]
    a["denseT"] = inputs["dense_ctx"].reshape(B // 128, Q, GR, -1).transpose(3, 0, 2, 1).reshape(-1, B)
    a["W1"] = inputs["L0_rec_W1"]
    a["W2t"] = inputs["L0_rec_W2"].transpose(1, 2, 0)
    a["b12"] = np.stack([inputs["L0_rec_b1"], inputs["L0_rec_b2"]], axis=1)
    a["W_top1"] = inputs["W_top1"]
    a["W_top2"] = inputs["W_top2"]
    a["W_top3p"] = inputs["W_top3"].reshape(-1, 128).T
    a["b_top"] = np.concatenate([inputs["b_top1"].reshape(-1, 128), inputs["b_top2"].reshape(-1, 128)]).T
    a["ident"] = np.eye(128, dtype=np.float32)
    a = {k: np.ascontiguousarray(v) for k, v in a.items()}

    nc = bacc.Bacc("TRN2", target_bir_lowering=False, num_devices=1)
    t = {k: nc.dram_tensor(f"in_{k}", v.shape, mybir.dt.from_np(v.dtype), kind="ExternalInput").ap()
         for k, v in a.items()}
    t["y"] = nc.dram_tensor("out_y", (1, B), F32, kind="ExternalOutput").ap()
    build_dlrm_tower(nc, t)
    r = run_bass_kernel_spmd(nc, [{f"in_{k}": v for k, v in a.items()}], core_ids=[0])
    return r.results[0]["out_y"].reshape(B, 1)
```

```python
from contextlib import ExitStack

import concourse.bass as bass
from concourse import mybir

F32 = mybir.dt.float32
I32 = mybir.dt.int32
ALU = mybir.AluOpType
ACT = mybir.ActivationFunctionType


def tri(n):
    return n * (n + 1) // 2


def build_dlrm_tower(nc, t):
    B, F = t["ids"].shape
    K = t["tbl_0"].shape[1]
    H = t["W1"].shape[0]
    DC = t["denseT"].shape[0]
    N1 = t["W_top1"].shape[1]
    N2 = t["W_top2"].shape[1]
    Q = 128 // K
    TILE = 128
    GR = TILE // Q
    HG = GR // 2
    CT = 2
    CB = CT * TILE
    CHUNKS = B // CB
    LAST = CHUNKS - 1
    QUAD = 4
    QT = GR // QUAD
    QC = CT * QT
    QH = HG // QUAD

    FH = F // 2
    LOW = 4
    NP = F + 1
    CONST = FH
    HI = tri(FH) - tri(LOW)
    ROW_AHI = FH + 1
    ROW_ALO = ROW_AHI + HI
    ROW_BLO = ROW_ALO + tri(LOW)
    ROW_BHI = ROW_BLO + tri(LOW)
    ROWS = ROW_BHI + HI
    Y_ROWS = ROW_BHI
    X_ROWS = ROWS - ROW_ALO
    COLS = NP - LOW
    HH = FH * FH
    W1N = 3 * HH + 1
    CU = -(-FH // 4)

    NX, NM = FH + 1, FH - LOW
    merged = []
    m = 0
    while m < NM:
        n = m + 1
        while n < NM and FH + 1 + tri(LOW + n + 1) - tri(LOW) <= X_ROWS - (tri(FH - m) - tri(LOW)):
            n += 1
        merged.append((m, n, FH + 1 + tri(LOW + n) - tri(LOW)))
        assert merged[-1][2] <= X_ROWS - (tri(FH - m) - tri(LOW))
        m = n

    UX, UM, UY = 0, NX, NX + NM
    UZ_X, UZ_Y, UZ_C = NX - 1, UY + NX, UY + NX + 1
    UNITS = UZ_C + CU

    def pos(f):
        return f if f < FH else f + 1

    def block(half, q):
        return (0, q, q) if half == 0 else (F - 1 - q, F - 1, F - 1 - q)

    def row(half, q):
        if half == 0:
            return ROW_ALO + tri(q) if q < LOW else ROW_AHI + tri(q) - tri(LOW)
        return ROW_BLO + tri(q) if q < LOW else ROW_BHI + tri(FH) - tri(q + 1)

    with ExitStack() as ctx:
        def sb(name, shape, dt=F32):
            return ctx.enter_context(nc.sbuf_tensor(name, shape, dt))

        def bank(name):
            return ctx.enter_context(nc.psum_tensor(name, [128, 512], F32))

        def sem(name):
            return ctx.enter_context(nc.semaphore(name))

        idx = sb("idx", [128, CT, F], I32)
        emb = sb("emb", [128, CT, NP, K])
        embT = sb("embT", [128, CT, NP, GR])
        HT = 2 * CT
        P01 = sb("P01", [128, 2, HG, ROWS])
        M = sb("M", [128, HT, HG, Q, NP])
        wz = sb("wz", [128, UNITS, H])
        w1 = sb("w1", [128, F, F])
        w1s = sb("w1s", [128, W1N])
        w2t = sb("w2t", [128, F, H])
        b12 = sb("b12", [128, 2])
        ident = sb("ident", [128, 128])
        wt1 = sb("wt1", [128, 3, N1])
        wt2 = sb("wt2", [128, N1 // 128, N2])
        wt3 = sb("wt3", [128, N2 // 128])
        bt = sb("bt", [128, N1 // 128 + N2 // 128])
        dense = sb("dense", [DC, B])
        yrow = sb("yrow", [1, B])
        Dbuf = sb("Dbuf", [128, F * W1N])
        D = Dbuf[:, :].rearrange("h (x c) -> h x c", x=F)
        Dsame = [D[:, :, k * HH:(k + 1) * HH].rearrange("h x (y z) -> h x y z", y=FH) for k in range(2)]
        Dab = D[:, :, 2 * HH:3 * HH].rearrange("h x (y z) -> h x y z", y=FH)
        TN = (2 * NX + NM) * CB
        assert TN <= F * W1N
        T = Dbuf[:, 0:TN].rearrange("p (j b) -> p j b", b=CB)
        TX, TM, TY = T[:, 0:NX, :], T[:, NX:NX + NM, :], T[:, NX + NM:2 * NX + NM, :]
        w2flat = w2t[:, :, :].rearrange("i x h -> i (x h)")
        TC = w2flat[:, 0:CU * CB].rearrange("p (u b) -> p u b", u=CU)
        o = CU * CB
        zs = w2flat[:, o:o + 2 * CB].rearrange("p (z b) -> p z b", z=2)
        o += 2 * CB
        h1 = w2flat[:, o:o + N1 // 128 * CB].rearrange("p (m b) -> p m b", b=CB)
        o += N1 // 128 * CB
        h2 = w2flat[:, o:o + N2 // 128 * CB].rearrange("p (m b) -> p m b", b=CB)
        assert o + N2 // 128 * CB <= F * H
        SY, SX = (NX + 1) * Y_ROWS, (NX + NM) * X_ROWS
        staging = sb("staging", [128, SY + SX + CU * 128])
        stY = staging[:, 0:SY].rearrange("h (u r) -> h u r", r=Y_ROWS)
        stX = staging[:, SY:SY + SX].rearrange("h (u r) -> h u r", r=X_ROWS)
        stM = stX[:, NX:NX + NM, :]
        stC = staging[:, SY + SX:SY + SX + CU * 128].rearrange("h (u r) -> h u r", u=CU)
        PN = HG * ROWS
        assert HT == 4 and TN + PN <= F * W1N and PN <= SY + SX + CU * 128
        P = [P01[:, 0, :, :], P01[:, 1, :, :], Dbuf[:, TN:TN + PN].rearrange("p (r n) -> p r n", r=HG),
             staging[:, 0:PN].rearrange("p (r n) -> p r n", r=HG)]

        psT = [bank(f"psT{i}") for i in range(4)]
        psZ = bank("psZ")
        psH = [bank(f"psH{i}") for i in range(2)]
        psO = bank("psO")

        w_in = sem("w_in")
        w2_in = [sem(f"w2_in{i}") for i in range(2)]
        mlp_in = sem("mlp_in")
        idx_in = [sem(f"idx_in{i}") for i in range(CT)]
        gathered = [sem(f"gathered{i}") for i in range(CT)]
        slot_free = sem("slot_free")
        ones_set = sem("ones_set")
        ident_in = sem("ident_in")
        transposed = sem("transposed")
        prepared = sem("prepared")
        moments = sem("moments")
        kept = sem("kept")
        x_kept = sem("x_kept")
        crossed = sem("crossed")
        z_done = sem("z_done")
        z_kept = sem("z_kept")
        h1_done = sem("h1_done")
        h1_kept = sem("h1_kept")
        h2_done = sem("h2_done")
        h2_kept = sem("h2_kept")
        y_done = sem("y_done")
        y_kept = sem("y_kept")
        stored = sem("stored")
        w1_sym = sem("w1_sym")
        d_done = sem("d_done")
        d_kept = sem("d_kept")
        st_step = sem("st_step")
        wz_done = sem("wz_done")
        wz_kept = sem("wz_kept")
        cross_zero = sem("cross_zero")

        ALL = slice(0, CB)

        def tile_w(i):
            return slice(i * TILE, i * TILE + TILE)

        staged = {}

        block_ = ctx.enter_context(nc.Block())

        assert W1N <= 512
        wz_sets = []
        for stage, unit, n, rows in ((stY, UY, NX + 1, Y_ROWS), (stX, UX, NX + NM, X_ROWS), (stC, UZ_C, CU, 128)):
            wz_sets += [(stage, a, unit + a, min(4, n - a), rows) for a in range(0, n, 4)]
        Y_SETS = -(-(NX + 1) // 4)

        @block_.sync
        def _(sp):
            for i in range(CT):
                sp.dma_start(idx[:, i, :], t["ids"][i * TILE:(i + 1) * TILE, :]).then_inc(idx_in[i], 16)
            sp.dma_start(w2t[:, 0:FH, :], t["W2t"][:, 0:FH, :]).then_inc(w2_in[0], 16)
            sp.dma_start(w2t[:, FH:F, :], t["W2t"][:, FH:F, :]).then_inc(w2_in[1], 16)
            sp.dma_start(ident[:, :], t["ident"]).then_inc(ident_in, 16)
            sp.dma_start(wt1[:, 0:2, :], t["W_top1"][0:2 * H, :].rearrange("(c p) n -> p c n", p=H)).then_inc(mlp_in, 16)
            sp.dma_start(wt1[0:DC, 2, :], t["W_top1"][2 * H:2 * H + DC, :]).then_inc(mlp_in, 16)
            sp.dma_start(wt2[:, :, :], t["W_top2"].rearrange("(c p) n -> p c n", p=128)).then_inc(mlp_in, 16)
            sp.dma_start(wt3[:, :], t["W_top3p"]).then_inc(mlp_in, 16)
            sp.dma_start(bt[:, :], t["b_top"]).then_inc(mlp_in, 16)
            sp.dma_start(dense[:, :], t["denseT"]).then_inc(mlp_in, 16)
            with sp.Fori(0, CHUNKS - 1) as c:
                for i in range(CT):
                    sp.wait_ge(gathered[i], c * (16 * F) + 16 * F)
                    sp.dma_start(idx[:, i, :],
                                 t["ids"][bass.ds(c * CB + (CB + i * TILE), TILE), :]).then_inc(idx_in[i], 16)
            sp.wait_ge(y_kept, LAST + CT)
            sp.dma_start(t["y"], yrow[:, :]).then_inc(stored, 16)
            sp.wait_ge(stored, 16)

        @block_.gpsimd
        def _(pool):
            def gather(c, first):
                for i in range(CT):
                    if not first:
                        pool.wait_ge(idx_in[i], 16 * c + 16)
                        pool.wait_ge(transposed, CT * c - (CT - 1 - i))
                        pool.sem_inc(slot_free, 1)
                    else:
                        pool.wait_ge(idx_in[i], 16)
                    for f in range(F):
                        pool.indirect_dma_start(
                            out=emb[:, i, pos(f), :], out_offset=None, in_=t[f"tbl_{f}"],
                            in_offset=bass.IndirectOffsetOnAxis(ap=idx[:, i, f:f + 1], axis=0),
                        ).then_inc(gathered[i], 16)

            gather(0, True)
            with pool.Fori(1, CHUNKS) as c:
                gather(c, False)

        @block_.vector
        def _(dve):
            steps = [0]

            def step(ins):
                steps[0] += 1
                ins.then_inc(st_step, 1)

            def settle():
                dve.wait_ge(st_step, steps[0])

            dve.wait_ge(w_in, 32)
            wsame = [w1s[:, k * HH:(k + 1) * HH].rearrange("i (y z) -> i y z", y=FH) for k in range(2)]
            wab = w1s[:, 2 * HH:3 * HH].rearrange("i (y z) -> i y z", y=FH)
            for out, y, z in ((wsame[0], 0, 0), (wsame[1], FH, FH), (wab, 0, FH)):
                step(nc.vector.tensor_tensor(out, w1[:, y:y + FH, z:z + FH],
                                             w1[:, z:z + FH, y:y + FH].rearrange("i z y -> i y z"), ALU.add))
            settle()
            w1flat = w1[:, :, :].rearrange("i y z -> i (y z)")
            for k in range(2):
                first = k * FH * (F + 1)
                step(nc.vector.tensor_copy(w1s[:, k * HH:k * HH + HH:FH + 1],
                                           w1flat[:, first:first + (FH - 1) * (F + 1) + 1:F + 1]))
            nc.vector.tensor_copy(w1s[:, 3 * HH:W1N], b12[:, 0:1]).then_inc(w1_sym, 1)

            nc.vector.memset(emb[:, :, CONST, :], 1.0).then_inc(ones_set, 1)
            for out in (staging, M):
                step(nc.vector.memset(out[:], 0.0))
            settle()

            def places(half, q, own, low_cols, stage, r0, unit0):
                lo, hi, s = block(half, q)
                h0 = half * FH
                if own:
                    f0, f1 = (LOW if not low_cols else 0, FH - 1) if half == 0 else \
                             (FH, F - 1 if low_cols else F - 1 - LOW)
                    a, b = (s, f1) if half == 0 else (f0, s)
                else:
                    f0, f1 = (FH, F - 1) if half == 0 else (0, FH - 1)
                    a, b = f0, f1
                r = row(half, q) - r0

                def out(a, b, lo_, hi_):
                    return stage[:, unit0 + a - f0:unit0 + b + 1 - f0, r + lo_ - lo:r + hi_ + 1 - lo]

                def t1(a, b, lo, hi):
                    return Dsame[half][:, a:b + 1, s - h0, lo - h0:hi + 1 - h0]

                def t2(a, b, lo, hi):
                    if own:
                        return Dsame[half][:, s, a - h0:b + 1 - h0, lo - h0:hi + 1 - h0]
                    if half == 0:
                        return Dab[:, s, lo:hi + 1, a - FH:b + 1 - FH].rearrange("h p j -> h j p")
                    return Dab[:, s, a:b + 1, lo - FH:hi + 1 - FH]

                def t3(a, b, lo, hi):
                    if own:
                        v = Dsame[half][:, lo:hi + 1, s - h0, a - h0:b + 1 - h0]
                    elif half == 0:
                        v = Dab[:, lo:hi + 1, s, a - FH:b + 1 - FH]
                    else:
                        v = Dab[:, lo:hi + 1, a:b + 1, s - FH]
                    return v.rearrange("h p j -> h j p")

                past = (a + 1, b) if half == 0 else (a, b - 1)
                less = (lo, hi - 1) if half == 0 else (lo + 1, hi)
                return out, t1, t2, t3, (a, b), past, (lo, hi), less, s

            def two_terms(rules):
                for rule in rules:
                    out, t1, t2, _, cols, past, pairs, _, s = places(*rule)
                    if rule[2]:
                        step(nc.vector.tensor_copy(out(s, s, *pairs), t1(s, s, *pairs)))
                        cols = past
                    if cols[1] >= cols[0]:
                        step(nc.vector.tensor_tensor(out(*cols, *pairs), t1(*cols, *pairs), t2(*cols, *pairs), ALU.add))

            def add_third(rules):
                for rule in rules:
                    out, _, _, t3, cols, _, _, less, _ = places(*rule)
                    if rule[1] > 0:
                        step(nc.vector.tensor_tensor(out(*cols, *less), out(*cols, *less), t3(*cols, *less), ALU.add))

            own_a = [(0, q, True, False, stM, 0, 0) for q in range(LOW, FH)] + \
                    [(0, q, True, True, stX, ROW_ALO, 0) for q in range(LOW)]
            a_b = [(0, q, False, True, stY, 0, 1) for q in range(FH)]
            own_b = [(1, q, True, True, stY, 0, 1) for q in range(LOW)] + \
                    [(1, q, True, False, stM, ROW_ALO, 0) for q in range(LOW, FH)]
            b_a = [(1, q, False, True, stX, ROW_ALO, 0) for q in range(FH)]

            dve.wait_ge(d_kept, FH)
            two_terms(own_a)
            for rule in a_b:
                out, _, t2, t3, cols, _, _, less, s = places(*rule)
                step(nc.vector.tensor_copy(out(*cols, s, s), t2(*cols, s, s)))
                if rule[1] > 0:
                    step(nc.vector.tensor_tensor(out(*cols, *less), t2(*cols, *less), t3(*cols, *less), ALU.add))
            settle()
            add_third(own_a)
            step(nc.vector.tensor_copy(stY[:, 0, 0:FH], D[:, 0:FH, 3 * HH]))
            step(nc.vector.tensor_copy(stY[:, 0, CONST:CONST + 1], b12[:, 1:2]))
            step(nc.vector.tensor_copy(stY[:, NX, CONST:CONST + 1], b12[:, 0:1]))
            for q in range(FH):
                r = row(0, q)
                step(nc.vector.tensor_copy(stY[:, NX, r:r + q + 1], wsame[0][:, q, 0:q + 1]))
                r = row(1, q) - ROW_ALO
                step(nc.vector.tensor_copy(stX[:, CONST, r:r + q + 1], wsame[1][:, FH - 1 - q, FH - 1 - q:FH]))
            for m in range(4):
                n = len(range(m, FH, 4))
                step(nc.vector.tensor_copy(stC[:, 0:n, 32 * m:32 * m + FH],
                                           wab[:, :, m:m + 4 * (n - 1) + 1:4].rearrange("h a u -> h u a")))

            dve.wait_ge(d_kept, F)
            for rule in a_b:
                out, t1, _, _, cols, _, pairs, _, _ = places(*rule)
                step(nc.vector.tensor_tensor(out(*cols, *pairs), out(*cols, *pairs), t1(*cols, *pairs), ALU.add))
            two_terms(own_b)
            step(nc.vector.tensor_copy(stY[:, 1:NX, CONST], D[:, FH:F, 3 * HH]))
            two_terms(b_a)
            settle()
            add_third(own_b[:LOW])
            settle()
            staged["Y"] = steps[0]
            add_third(own_b[LOW:])
            add_third(b_a)
            settle()
            staged["X"] = steps[0]
            nc.vector.memset(TC[:, :, :], 0.0).then_inc(cross_zero, 1)

            def tile_of(c, i, first):
                dve.wait_ge(gathered[i], c * (16 * F) + 16 * F)
                if first and i == 0:
                    dve.wait_ge(ones_set, 1)
                nc.vector.transpose(embT[:, i, :, :].rearrange("p a b -> p (a b)"),
                                    emb[:, i, :, :].rearrange("p a b -> p (a b)")).then_inc(transposed, 1)
                dve.wait_ge(transposed, c * CT + i + 1)
                for hf in range(2):
                    n = i * 2 + hf
                    if not first:
                        dve.wait_ge(moments, QC * c - QC + QH * (n + 1))
                    g0, g1 = hf * HG, hf * HG + HG
                    nc.vector.tensor_copy(P[n][:, :, 0:FH + 1],
                                          embT[:, i, 0:FH + 1, g0:g1].rearrange("p f r -> p r f"))
                    for q4 in range(Q):
                        s = slice(32 * q4, 32 * q4 + 32)
                        nc.vector.tensor_copy(M[s, n, :, q4, :],
                                              embT[s, i, :, g0:g1].rearrange("p f r -> p r f"))
                    for half in range(2):
                        for q in range(FH):
                            lo, hi, s = (pos(x) for x in block(half, q))
                            w = hi - lo + 1
                            r = row(half, q)
                            last = nc.vector.tensor_tensor(
                                P[n][:, :, r:r + w], embT[:, i, lo:hi + 1, g0:g1].rearrange("p f r -> p r f"),
                                embT[:, i, s:s + 1, g0:g1].rearrange("p f r -> p r f").to_broadcast([128, HG, w]),
                                ALU.mult)
                    last.then_inc(prepared, 1)

            def cross(c, n0, n1):
                dve.wait_ge(kept, QC * c + n1 * QT)
                if isinstance(c, int) and c == 0:
                    dve.wait_ge(cross_zero, 1)
                b = slice(n0 * TILE, n1 * TILE)
                for m in range(4):
                    n = len(range(m, FH, 4))
                    j = 1 + m
                    ins = nc.vector.tensor_copy(TC[32 * m:32 * m + FH + 1, 0:n, b],
                                                TY[0:FH + 1, j:j + 4 * (n - 1) + 1:4, b])
                ins.then_inc(crossed, 1)

            tile_of(0, 0, True)
            dve.wait_ge(wz_done, len(wz_sets))
            tile_of(0, 1, True)
            cross(0, 0, CT)
            with dve.Fori(1, LAST) as c:
                for i in range(CT):
                    tile_of(c, i, False)
                cross(c, 0, CT)
            for i in range(CT):
                tile_of(LAST, i, False)
                cross(LAST, i, i + 1)

        @block_.tensor
        def _(pe):
            pe.wait_ge(w1_sym, 1)
            for x in range(F):
                if x % FH == 0:
                    pe.wait_ge(w2_in[x // FH], 16)
                if x >= 4:
                    pe.wait_ge(d_kept, x - 3)
                nc.tensor.matmul(psT[x % 4][:, 0:W1N], w2t[:, x, :], w1s[:, :],
                                 start=True, stop=True).then_inc(d_done, 1)

            pe.wait_ge(ident_in, 16)
            for n, (stage, a, _, units, rows) in enumerate(wz_sets):
                pe.wait_ge(st_step, staged["Y" if n < Y_SETS else "X"])
                if n >= 2:
                    pe.wait_ge(wz_kept, n - 1)
                for k in range(units):
                    last = nc.tensor.transpose(psH[n % 2][0:rows, k * H:k * H + H], stage[:, a + k, :], ident[:, :])
                last.then_inc(wz_done, 1)

            def moments_of(c, tiles=range(CT)):
                for n in range(2 * tiles[0], 2 * tiles[-1] + 2):
                    pe.wait_ge(prepared, 2 * CT * c + n + 1)
                    for m in range(QH):
                        k = n * QH + m
                        if not (isinstance(c, int) and k < 2):
                            pe.wait_ge(kept, QC * c + k - 1)
                        for g in range(QUAD):
                            r = m * QUAD + g
                            cols = slice(g * Q * COLS, (g + 1) * Q * COLS)
                            nc.tensor.matmul(psT[k % 2][0:Y_ROWS, cols], P[n][:, r, 0:Y_ROWS],
                                             M[:, n, r, :, LOW:NP], start=True, stop=True)
                            last = nc.tensor.matmul(psT[2 + k % 2][0:X_ROWS, cols], P[n][:, r, ROW_ALO:ROWS],
                                                    M[:, n, r, :, 0:COLS], start=True, stop=True)
                        last.then_inc(moments, 1)

            z2_units = [(UX + u, X_ROWS, TX[0:X_ROWS, u, :]) for u in range(FH)]
            z2_units += [(UM + u, X_ROWS, TM[0:X_ROWS, u, :]) for u in range(NM)]
            z2_units += [(UY + u, Y_ROWS, TY[0:Y_ROWS, u, :]) for u in range(NX)]
            z1_units = [(UZ_Y, Y_ROWS, TY[0:Y_ROWS, 0, :]), (UZ_X, X_ROWS, TX[0:X_ROWS, CONST, :])]
            z1_units += [(UZ_C + u, 128, TC[:, u, :]) for u in range(CU)]
            z2_half = len(z2_units) // 2


            def z2_first(turn, w, quads):
                pe.wait_ge(kept, quads)
                for n, (unit, rows, rhs) in enumerate(z2_units[:z2_half]):
                    nc.tensor.matmul(psZ[:, CB + w.start:CB + w.stop], wz[0:rows, unit, :], rhs[:, w],
                                     start=(n == 0), stop=False)

            def z2_second(turn, w):
                for n, (unit, rows, rhs) in enumerate(z2_units[z2_half:], z2_half):
                    nc.tensor.matmul(psZ[:, CB + w.start:CB + w.stop], wz[0:rows, unit, :], rhs[:, w],
                                     start=False, stop=(n == len(z2_units) - 1))

            def z1_of(turn, w):
                pe.wait_ge(crossed, turn + 1)
                for n, (unit, rows, rhs) in enumerate(z1_units):
                    last = nc.tensor.matmul(psZ[:, w], wz[0:rows, unit, :], rhs[:, w],
                                            start=(n == 0), stop=(n == len(z1_units) - 1))
                last.then_inc(z_done, 1)

            def layer1(c, w, b0):
                pe.wait_ge(z_kept, c + 1)
                if not (isinstance(c, int) and c == 0):
                    pe.wait_ge(h2_kept, N2 // 128 * c)
                for m in range(N1 // 128):
                    out = psH[m // 2][:, m % 2 * CB + w.start:m % 2 * CB + w.stop]
                    cols = slice(m * 128, m * 128 + 128)
                    nc.tensor.matmul(out, wt1[:, 0, cols], zs[:, 0, w], start=True, stop=False)
                    nc.tensor.matmul(out, wt1[:, 1, cols], zs[:, 1, w], start=False, stop=False)
                    nc.tensor.matmul(out, wt1[0:DC, 2, cols], dense[:, bass.ds(b0, w.stop - w.start)],
                                     start=False, stop=True).then_inc(h1_done, 1)

            def layer2(c, w):
                for m in range(N2 // 128):
                    for k in range(N1 // 128):
                        if m == 0:
                            pe.wait_ge(h1_kept, N1 // 128 * c + max(k + 1, 2))
                        last = nc.tensor.matmul(psH[0][:, m * CB + w.start:m * CB + w.stop],
                                                wt2[:, k, m * 128:m * 128 + 128], h1[:, k, w], start=(k == 0), stop=(k == N1 // 128 - 1))
                    last.then_inc(h2_done, 1)

            def layer3(c, w):
                pe.wait_ge(h2_kept, N2 // 128 * c + N2 // 128)
                if not (isinstance(c, int) and c == 0):
                    pe.wait_ge(y_kept, c)
                for k in range(N2 // 128):
                    last = nc.tensor.matmul(psO[0:1, w], wt3[:, k:k + 1], h2[:, k, w],
                                            start=(k == 0), stop=(k == N2 // 128 - 1))
                last.then_inc(y_done, 1)

            pe.wait_ge(d_kept, F)
            pe.wait_ge(wz_kept, len(wz_sets))
            pe.wait_ge(mlp_in, 6 * 16)
            moments_of(0)
            z2_first(0, ALL, QC)
            z2_second(0, ALL)
            z1_of(0, ALL)

            def round_(c, before, b0_before):
                moments_of(c, range(CT - 1))
                layer1(before, ALL, b0_before)
                moments_of(c, range(CT - 1, CT))
                layer2(before, ALL)
                z2_first(c, ALL, QC * c + QC)
                layer3(before, ALL)
                z2_second(c, ALL)
                z1_of(c, ALL)

            round_(1, 0, 0)
            with pe.Fori(2, LAST) as c:
                round_(c, c - 1, c * CB - CB)
            before = (LAST - 1, ALL, CB * (LAST - 1))
            for i in range(CT):
                turn, w = LAST + i, tile_w(i)
                if i == 0:
                    moments_of(LAST, range(1))
                    layer1(*before)
                else:
                    layer1(*before)
                    moments_of(LAST, range(i, i + 1))
                layer2(before[0], before[1])
                z2_first(turn, w, QC * LAST + QT * (i + 1))
                layer3(before[0], before[1])
                z2_second(turn, w)
                z1_of(turn, w)
                before = (turn, w, CB * LAST + i * TILE)
            layer1(*before)
            layer2(before[0], before[1])
            layer3(before[0], before[1])

        @block_.scalar
        def _(act):
            act.dma_start(w1[:, :, :], t["W1"]).then_inc(w_in, 16)
            act.dma_start(b12[:, :], t["b12"]).then_inc(w_in, 16)
            for x in range(F):
                act.wait_ge(d_done, x + 1)
                nc.scalar.activation(D[:, x, :], psT[x % 4][:, 0:W1N], ACT.Copy).then_inc(d_kept, 1)
            for n, (_, _, unit, units, rows) in enumerate(wz_sets):
                act.wait_ge(wz_done, n + 1)
                nc.scalar.activation(wz[0:rows, unit:unit + units, :],
                                     psH[n % 2][0:rows, 0:units * H].rearrange("p (u h) -> p u h", h=H),
                                     ACT.Copy).then_inc(wz_kept, 1)

            def keep_moments(c, tiles=range(CT)):
                for k in range(QT * tiles[0], QT * tiles[-1] + QT):
                    act.wait_ge(moments, QC * c + k + 1)
                    b = slice(k * QUAD * Q, (k + 1) * QUAD * Q)
                    Y, X = (ps[:, 0:QUAD * Q * COLS].rearrange("p (x j) -> p j x", j=COLS)
                            for ps in (psT[k % 2], psT[2 + k % 2]))
                    nc.scalar.activation(T[0:X_ROWS, 0:COLS, b], X[0:X_ROWS, :, :], ACT.Copy).then_inc(x_kept, 1)
                    nc.scalar.activation(TY[0:Y_ROWS, :, b], Y[0:Y_ROWS, NM:COLS, :], ACT.Copy)
                    act.wait_ge(x_kept, QC * c + k + 1)
                    for m0, m1, rows in merged:
                        last = nc.scalar.activation(TM[0:rows, m0:m1, b], Y[0:rows, m0:m1, :], ACT.Copy)
                    last.then_inc(kept, 1)

            def keep_z(c, w):
                act.wait_ge(z_done, c + 1)
                nc.scalar.activation(zs[:, :, w], psZ[:, :].rearrange("p (z b) -> p z b", z=2)[:, :, w],
                                     ACT.Copy).then_inc(z_kept, 1)

            def keep_h1(c, w):
                for m in range(N1 // 128):
                    act.wait_ge(h1_done, N1 // 128 * c + m // 2 * 2 + 2)
                    nc.scalar.activation(h1[:, m, w], psH[m // 2][:, m % 2 * CB + w.start:m % 2 * CB + w.stop], ACT.Relu,
                                         bias=bt[:, m:m + 1]).then_inc(h1_kept, 1)

            def keep_h2(c, w):
                act.wait_ge(h2_done, N2 // 128 * c + N2 // 128)
                for m in range(N2 // 128):
                    nc.scalar.activation(h2[:, m, w], psH[0][:, m * CB + w.start:m * CB + w.stop], ACT.Relu,
                                         bias=bt[:, N1 // 128 + m:N1 // 128 + m + 1]).then_inc(h2_kept, 1)

            def keep_y(c, w, b0):
                act.wait_ge(y_done, c + 1)
                nc.scalar.activation(
                    yrow[0:1, bass.ds(b0, w.stop - w.start)].rearrange("o (t q r) -> o t r q", q=Q, r=GR),
                    psO[0:1, w].rearrange("o (t r q) -> o t r q", q=Q, r=GR), ACT.Copy).then_inc(y_kept, 1)

            act.wait_ge(mlp_in, 6 * 16)
            act.wait_ge(st_step, staged["X"])
            keep_moments(0)
            keep_z(0, ALL)
            with act.Fori(1, LAST) as c:
                keep_moments(c, range(CT - 1))
                keep_h1(c - 1, ALL)
                keep_moments(c, range(CT - 1, CT))
                keep_h2(c - 1, ALL)
                keep_y(c - 1, ALL, c * CB - CB)
                keep_z(c, ALL)
            before = (LAST - 1, ALL, CB * (LAST - 1))
            for i in range(CT):
                if i == 0:
                    keep_moments(LAST, range(1))
                    keep_h1(before[0], before[1])
                else:
                    keep_h1(before[0], before[1])
                    keep_moments(LAST, range(i, i + 1))
                keep_h2(before[0], before[1])
                keep_y(*before)
                keep_z(LAST + i, tile_w(i))
                before = (LAST + i, tile_w(i), CB * LAST + i * TILE)
            keep_h1(before[0], before[1])
            keep_h2(before[0], before[1])
            keep_y(*before)


def kernel(**inputs):
    import numpy as np
    import concourse.bacc as bacc
    from concourse.bass_utils import run_bass_kernel_spmd

    B, F = inputs["ids"].shape
    K = inputs["tbl_0"].shape[1]
    Q, GR = 128 // K, 128 // (128 // K)
    a = {f"tbl_{f}": inputs[f"tbl_{f}"] for f in range(F)}
    a["ids"] = inputs["ids"]
    a["denseT"] = inputs["dense_ctx"].reshape(B // 128, Q, GR, -1).transpose(3, 0, 2, 1).reshape(-1, B)
    a["W1"] = inputs["L0_rec_W1"]
    a["W2t"] = inputs["L0_rec_W2"].transpose(1, 2, 0)
    a["b12"] = np.stack([inputs["L0_rec_b1"], inputs["L0_rec_b2"]], axis=1)
    a["W_top1"] = inputs["W_top1"]
    a["W_top2"] = inputs["W_top2"]
    a["W_top3p"] = inputs["W_top3"].reshape(-1, 128).T
    a["b_top"] = np.concatenate([inputs["b_top1"].reshape(-1, 128), inputs["b_top2"].reshape(-1, 128)]).T
    a["ident"] = np.eye(128, dtype=np.float32)
    a = {k: np.ascontiguousarray(v) for k, v in a.items()}

    nc = bacc.Bacc("TRN2", target_bir_lowering=False, num_devices=1)
    t = {k: nc.dram_tensor(f"in_{k}", v.shape, mybir.dt.from_np(v.dtype), kind="ExternalInput").ap()
         for k, v in a.items()}
    t["y"] = nc.dram_tensor("out_y", (1, B), F32, kind="ExternalOutput").ap()
    build_dlrm_tower(nc, t)
    r = run_bass_kernel_spmd(nc, [{f"in_{k}": v for k, v in a.items()}], core_ids=[0])
    return r.results[0]["out_y"].reshape(B, 1)
```

```python
from contextlib import ExitStack

import concourse.bass as bass
from concourse import mybir

F32 = mybir.dt.float32
I32 = mybir.dt.int32
F16 = mybir.dt.float16
BF16 = mybir.dt.bfloat16
ALU = mybir.AluOpType
ACT = mybir.ActivationFunctionType


N_ONE_HOT = ((3, 3), (2, 3))


def tri(n):
    return n * (n + 1) // 2


def build_dlrm_tower(nc, t):
    B, F = t["ids"].shape
    K = t["tbl_0"].shape[1]
    H = t["W1"].shape[0]
    DC = t["denseT"].shape[0]
    N1 = t["W_top1"].shape[1]
    N2 = t["W_top2"].shape[1]
    Q = 128 // K
    TILE = 128
    GR = TILE // Q
    HG = GR // 2
    CT = 2
    CB = CT * TILE
    CHUNKS = B // CB
    LAST = CHUNKS - 1
    QUAD = 4
    QT = GR // QUAD
    QC = CT * QT
    QH = HG // QUAD

    FH = F // 2
    LOW_A, LOW_B = 2, 3
    NP = F + 1
    CONST = FH
    HI_A, HI_B = (tri(FH) - tri(low) for low in (LOW_A, LOW_B))
    ROW_AHI = 0
    ROW_G = ROW_AHI + HI_A
    ROW_ALO = ROW_G + FH + 1
    ROW_BLO = ROW_ALO + tri(LOW_A)
    ROW_BHI = ROW_BLO + tri(LOW_B)
    ROWS = ROW_BHI + HI_B
    Y_ROWS = ROW_BHI
    X_ROWS = 96
    ROW_X = ROWS - X_ROWS
    assert ROW_X <= ROW_ALO and ROW_G + FH + 1 <= Y_ROWS <= 128
    YC, XC = NP - LOW_A, NP - LOW_B
    HH = FH * FH
    W1N = 3 * HH + 1

    CORNER = 128 - X_ROWS
    NX = FH + 1
    NA = sum(tri(j + 1) - tri(LOW_A) <= CORNER + 1 for j in range(LOW_A, FH))
    NB = sum(tri(j + 1) - tri(LOW_B) <= CORNER for j in range(LOW_B, FH))
    NM = FH - LOW_B - NB
    M_LOW = sum(tri(FH - m) - tri(LOW_B) > X_ROWS - CORNER for m in range(NM))
    A_ROWS = [tri(FH - NM + m + 1) - tri(LOW_A) for m in range(NM)]
    assert tri(LOW_A + NA) - tri(LOW_A) == CORNER + 1 and LOW_A > 0 and LOW_A + NA == FH - NM == FH - NB
    assert NB == NM and X_ROWS == 3 * CORNER
    assert all(n <= 128 - (tri(FH - m) - tri(LOW_B)) for m, n in enumerate(A_ROWS))

    UX, UM, UY, UZ = 0, FH, FH + NM, FH + NM + NX
    UNITS = UZ + 3

    free = [(2, 0, 128), (0, Y_ROWS, 128 - Y_ROWS), (1, X_ROWS, 128 - X_ROWS), (1, 0, ROW_BLO - ROW_X)]
    crossing = []
    u, r, left = free.pop(0)
    for b in range(FH):
        a = 0
        while a < FH:
            if left == 0:
                u, r, left = free.pop(0)
            n = min(FH - a, left)
            crossing.append((b, a, n, u, r))
            a, r, left = a + n, r + n, left - n

    OC = 8
    ONE_HOT = [f for f in range(F) if t[f"tbl_{f}"].shape[0] == 1000][:max(map(max, N_ONE_HOT))]
    OR = 1000 // OC
    NO = len(ONE_HOT)

    def is_chunk(c, number):
        return isinstance(c, int) and c == number

    def is_last_tile(c, i):
        return is_chunk(c, LAST) and i == CT - 1

    def looked(c, i):
        if is_last_tile(c, i):
            return []
        return list(enumerate(ONE_HOT[:N_ONE_HOT[0 if is_chunk(c, 0) else 1][i]]))

    def gathers_to(c, i):
        first, later = (16 * (F - n[i]) for n in N_ONE_HOT)
        if is_chunk(c, 0):
            return first
        if is_last_tile(c, i):
            return first + (LAST - 1) * later + 16 * F
        return c * later + first

    def ids_to(c, i):
        first, later = (16 * n[i] for n in N_ONE_HOT)
        return first if is_chunk(c, 0) else c * later + first

    def pos(f):
        return f if f < FH else f + 1

    def block(half, q):
        return (0, q, q) if half == 0 else (F - 1 - q, F - 1, F - 1 - q)

    def row(half, q):
        if half == 0:
            return ROW_ALO + tri(q) if q < LOW_A else ROW_AHI + tri(q) - tri(LOW_A)
        return ROW_BLO + tri(q) if q < LOW_B else ROW_BHI + tri(FH) - tri(q + 1)

    with ExitStack() as ctx:
        def sb(name, shape, dt=F32):
            return ctx.enter_context(nc.sbuf_tensor(name, shape, dt))

        def bank(name):
            return ctx.enter_context(nc.psum_tensor(name, [128, 512], F32))

        def sem(name):
            return ctx.enter_context(nc.semaphore(name))

        idx = sb("idx", [128, CT, F], I32)
        emb = sb("emb", [128, CT, NP, K])
        embT = sb("embT", [128, CT, NP, GR])
        HT = 2 * CT
        P01 = sb("P01", [128, 2, HG, ROWS])
        M = sb("M", [128, HT, HG, Q, NP])
        wz = sb("wz", [128, UNITS, H])
        w1 = sb("w1", [128, F, F])
        w1s = sb("w1s", [128, W1N])
        w2t = sb("w2t", [128, F, H])
        b12 = sb("b12", [128, 2])
        ident = sb("ident", [128, 128])
        ones = sb("ones", [128, 1])
        zero = sb("zero", [128, 1])
        wt1 = sb("wt1", [128, 3, N1])
        wt2 = sb("wt2", [128, N1 // 128, N2])
        wt3 = sb("wt3", [128, N2 // 128])
        bt = sb("bt", [128, N1 // 128 + N2 // 128])
        side = sb("side", [33, B])
        dense, yrow = side[0:DC, :], side[32:33, :]
        ids_all = sb("ids_all", [OR, CT, NO, TILE], I32)
        ids16 = sb("ids16", [OR, NO, TILE], F16)
        one_hot = sb("one_hot", [OR, NO, OC, TILE], BF16)
        parts = sb("parts", [OR, NO, OC, 3, K], BF16)
        row_of = sb("row_of", [OR, OC])
        tab32 = P01[0:OR, 0, :, :].rearrange("p r n -> p (r n)")[:, 0:NO * OC * K].rearrange(
            "p (f c k) -> p f c k", f=NO, c=OC)
        rest32 = P01[0:OR, 1, :, :].rearrange("p r n -> p (r n)")[:, 0:NO * OC * K].rearrange(
            "p (f c k) -> p f c k", f=NO, c=OC)
        Dbuf = sb("Dbuf", [128, F * W1N])
        D = Dbuf[:, :].rearrange("h (x c) -> h x c", x=F)
        Dsame = [D[:, :, k * HH:(k + 1) * HH].rearrange("h x (y z) -> h x y z", y=FH) for k in range(2)]
        Dab = D[:, :, 2 * HH:3 * HH].rearrange("h x (y z) -> h x y z", y=FH)
        TN = (2 * NX + NM) * CB
        assert TN <= F * W1N
        T = Dbuf[:, 0:TN].rearrange("p (j b) -> p j b", b=CB)
        TM, TX, TY = T[:, 0:NM, :], T[:, NM:NM + NX, :], T[:, NM + NX:NM + 2 * NX, :]
        w2flat = w2t[:, :, :].rearrange("i x h -> i (x h)")
        TC = w2flat[:, 0:CB]
        o = CB
        zs = w2flat[:, o:o + 2 * CB].rearrange("p (z b) -> p z b", z=2)
        o += 2 * CB
        h1 = w2flat[:, o:o + N1 // 128 * CB].rearrange("p (m b) -> p m b", b=CB)
        o += N1 // 128 * CB
        h2 = w2flat[:, o:o + N2 // 128 * CB].rearrange("p (m b) -> p m b", b=CB)
        o += N2 // 128 * CB
        h2w = w2flat[:, o:o + CB]
        assert N2 == 256 and o + CB <= F * H
        SIZES = dict(X=(FH, X_ROWS), M=(NM, 128), Y=(NX, Y_ROWS), Z=(3, 128), C=(FH, CORNER))
        SN = sum(u * r for u, r in SIZES.values())
        staging = sb("staging", [128, SN])
        staged_at, o = {}, 0
        for part, (u, r) in SIZES.items():
            staged_at[part] = staging[:, o:o + u * r].rearrange("h (u r) -> h u r", r=r)
            o += u * r
        stX, stM, stY, stZ, stC = staged_at.values()
        PN = HG * ROWS
        assert HT == 4 and TN + PN <= F * W1N and PN <= SN
        P = [P01[:, 0, :, :], P01[:, 1, :, :], Dbuf[:, TN:TN + PN].rearrange("p (r n) -> p r n", r=HG),
             staging[:, 0:PN].rearrange("p (r n) -> p r n", r=HG)]

        psT = [bank(f"psT{i}") for i in range(4)]
        psZ = bank("psZ")
        psH = [bank(f"psH{i}") for i in range(2)]
        psE = bank("psE")

        W2_CUTS = [0, 3, 9, 17, F]
        w_in = sem("w_in")
        w2_in = [sem(f"w2_in{i}") for i in range(len(W2_CUTS) - 1)]
        mlp_in = sem("mlp_in")
        idx_in = [sem(f"idx_in{i}") for i in range(CT)]
        gathered = [sem(f"gathered{i}") for i in range(CT)]
        slot_free = sem("slot_free")
        ones_set = sem("ones_set")
        m_zero = sem("m_zero")
        ident_in = sem("ident_in")
        transposed = sem("transposed")
        prepared = sem("prepared")
        x_moments = sem("x_moments")
        moments = sem("moments")
        kept = sem("kept")
        x_kept = sem("x_kept")
        crossed = sem("crossed")
        crossed_late = sem("crossed_late")
        tab_in = sem("tab_in")
        ids_in = [sem(f"ids_in{i}") for i in range(CT)]
        ids_cast = sem("ids_cast")
        one_hot_set = sem("one_hot_set")
        looked_up = sem("looked_up")
        summed = sem("summed")
        h2w_set = sem("h2w_set")
        z_done = sem("z_done")
        z_kept = sem("z_kept")
        h1_done = sem("h1_done")
        h1_kept = sem("h1_kept")
        h2_done = sem("h2_done")
        h2_kept = sem("h2_kept")
        y_done = sem("y_done")
        y_kept = sem("y_kept")
        stored = sem("stored")
        w1_sym = sem("w1_sym")
        d_done = sem("d_done")
        d_kept = sem("d_kept")
        st_step = sem("st_step")
        placed = sem("placed")
        m_first = sem("m_first")
        wz_done = sem("wz_done")
        wz_kept = sem("wz_kept")

        ALL = slice(0, CB)

        def tile_w(i):
            return slice(i * TILE, i * TILE + TILE)

        SHARE = len(crossing) // 3
        staged = {}

        block_ = ctx.enter_context(nc.Block())

        assert W1N <= 512
        wz_sets = []
        for stage, unit, n, rows, p0 in ((stY, UY, NX, Y_ROWS, 0), (stX, UX, FH, X_ROWS, 0), (stM, UM, NM, 128, 0),
                                         (stZ, UZ, 3, 128, 0), (stC, UX, FH, CORNER, X_ROWS)):
            wz_sets += [(stage, a, unit + a, min(4, n - a), rows, p0) for a in range(0, n, 4)]
        Y_SETS = -(-NX // 4)

        def spread(i, hf, q4):
            s = slice(K * q4, K * q4 + K)
            return M[s, 2 * i + hf, :, q4, :], embT[s, i, :, hf * HG:hf * HG + HG].rearrange("p f r -> p r f")

        def cross(eng, quads, w, pieces, signal):
            eng.wait_ge(kept, quads)
            for b, a, n, u, r in pieces:
                eng.dma_start((TY[r:r + n, 0, w], TX[r:r + n, CONST, w], TC[r:r + n, w])[u],
                              TY[ROW_G + a:ROW_G + a + n, 1 + b, w]).then_inc(signal, 16)

        def places(half, q, own, f0, f1, stage, row0, unit0):
            lo, hi, s = block(half, q)
            h0 = half * FH
            a, b = f0, f1
            if own:
                a, b = (max(s, f0), f1) if half == 0 else (f0, min(s, f1))
            r = row(half, q) - row0

            def out(a, b, lo_, hi_):
                return stage[:, unit0 + a - f0:unit0 + b + 1 - f0, r + lo_ - lo:r + hi_ + 1 - lo]

            def t1(a, b, lo, hi):
                return Dsame[half][:, a:b + 1, s - h0, lo - h0:hi + 1 - h0]

            def t2(a, b, lo, hi):
                if own:
                    return Dsame[half][:, s, a - h0:b + 1 - h0, lo - h0:hi + 1 - h0]
                if half == 0:
                    return Dab[:, s, lo:hi + 1, a - FH:b + 1 - FH].rearrange("h p j -> h j p")
                return Dab[:, s, a:b + 1, lo - FH:hi + 1 - FH]

            def t3(a, b, lo, hi):
                if own:
                    v = Dsame[half][:, lo:hi + 1, s - h0, a - h0:b + 1 - h0]
                elif half == 0:
                    v = Dab[:, lo:hi + 1, s, a - FH:b + 1 - FH]
                else:
                    v = Dab[:, lo:hi + 1, a:b + 1, s - FH]
                return v.rearrange("h p j -> h j p")

            with_q = own and a <= s <= b
            past = (a, b)
            if with_q:
                past = (a + 1, b) if half == 0 else (a, b - 1)
            less = (lo, hi - 1) if half == 0 else (lo + 1, hi)
            return out, t1, t2, t3, (a, b), past, with_q, (lo, hi), less, s

        A1, B1 = FH - NM, FH + NM
        own_a = [(0, q, True, A1, FH - 1, stM, 0, 0) for q in range(LOW_A, FH)] + \
                [(0, q, True, LOW_A, A1 - 1, stC, 0, LOW_A) for q in range(LOW_A, A1)] + \
                [(0, q, True, 0, FH - 1, stX, ROW_X, 0) for q in range(LOW_A)]
        a_b = [(0, q, False, FH, F - 1, stY, 0, 1) for q in range(FH)]
        own_b = [(1, q, True, FH, F - 1, stY, 0, 1) for q in range(LOW_B)] + \
                [(1, q, True, FH, B1 - 1, stM, ROW_X - CORNER, 0) for q in range(LOW_B, FH)] + \
                [(1, q, True, B1, F - 1 - LOW_B, stC, ROWS - CORNER, A1) for q in range(LOW_B, LOW_B + NB)]
        b_a = [(1, q, False, 0, FH - 1, stX, ROW_X, 0) for q in range(FH)]
        W1 = [w1s[:, k * HH:(k + 1) * HH].rearrange("i (y z) -> i y z", y=FH) for k in range(3)]
        places_a, places_all = [], []
        for todo, own, other in ((places_a, own_a, a_b), (places_all, own_b, [])):
            for rule in own:
                out, t1, _, _, _, _, with_q, pairs, less, s = places(*rule)
                if rule[5] is stC and rule[1] == A1 - 1 and own is own_a:
                    todo.append((stC[:, 0:1, 0:1], t1(s, s, s, s)))
                    pairs = less
                if with_q:
                    todo.append((out(s, s, *pairs), t1(s, s, *pairs)))
            if own is own_a:
                OWN_A = len(todo)
            for rule in other:
                out, _, t2, _, cols, _, _, _, _, s = places(*rule)
                todo.append((out(*cols, s, s), t2(*cols, s, s)))
        places_a.append((stY[:, 0, ROW_G:ROW_G + FH], D[:, 0:FH, 3 * HH]))
        places_all.append((stY[:, 1:NX, ROW_G + CONST], D[:, FH:F, 3 * HH]))
        places_z = [(st[:, 0, ROW_G + CONST:ROW_G + CONST + 1], b12[:, k:k + 1]) for st, k in ((stY, 1), (stZ, 0))]
        for q in range(FH):
            r = row(0, q)
            places_z.append((stZ[:, 0, r:r + q + 1], W1[0][:, q, 0:q + 1]))
            r = row(1, q) - ROW_X
            places_z.append((stZ[:, 1, r:r + q + 1], W1[1][:, FH - 1 - q, FH - 1 - q:FH]))
        for b, a, n, u, r in crossing:
            places_z.append((stZ[:, u, r:r + n], W1[2][:, a:a + n, b]))
        PER_X = -(-len(places_a) // (F - FH))
        PA, PALL = len(places_a), len(places_a) + len(places_all)

        @block_.sync
        def _(sp):
            def load_ids_all(c, i, b0):
                for n, f in looked(c, i):
                    sp.dma_start(ids_all[:, i, n, :],
                                 t["idsT"][f:f + 1, bass.ds(b0, TILE)].to_broadcast([OR, TILE])).then_inc(ids_in[i], 16)

            for i in range(CT):
                sp.dma_start(idx[:, i, :], t["ids"][i * TILE:(i + 1) * TILE, :]).then_inc(idx_in[i], 16)
            for a, b, loaded in zip(W2_CUTS, W2_CUTS[1:], w2_in):
                sp.dma_start(w2t[:, a:b, :], t["W2t"][:, a:b, :]).then_inc(loaded, 16)
            for n, f in enumerate(ONE_HOT):
                sp.dma_start(tab32[:, n, :, :],
                             t[f"tbl_{f}"].rearrange("(p c) k -> p c k", c=OC)).then_inc(tab_in, 16)
            sp.dma_start(row_of[:, :], t["row_of"]).then_inc(tab_in, 16)
            for i in range(CT):
                load_ids_all(0, i, i * TILE)
            sp.dma_start(ident[:, :], t["ident"]).then_inc(ident_in, 16)
            sp.dma_start(wt1[:, 0:2, :], t["W_top1"][0:2 * H, :].rearrange("(c p) n -> p c n", p=H)).then_inc(mlp_in, 16)
            sp.dma_start(wt1[0:DC, 2, :], t["W_top1"][2 * H:2 * H + DC, :]).then_inc(mlp_in, 16)
            sp.dma_start(wt2[:, :, :], t["W_top2"].rearrange("(c p) n -> p c n", p=128)).then_inc(mlp_in, 16)
            sp.dma_start(wt3[:, :], t["W_top3p"]).then_inc(mlp_in, 16)
            sp.dma_start(bt[:, :], t["b_top"]).then_inc(mlp_in, 16)
            sp.dma_start(dense[:, :], t["denseT"]).then_inc(mlp_in, 16)
            def next_indices(c):
                for i in range(CT):
                    sp.wait_ge(gathered[i], gathers_to(c, i))
                    sp.dma_start(idx[:, i, :],
                                 t["ids"][bass.ds(c * CB + (CB + i * TILE), TILE), :]).then_inc(idx_in[i], 16)
                    sp.wait_ge(ids_cast, c * CT + (i + 1))
                    load_ids_all(c + 1, i, c * CB + (CB + i * TILE))
                cross(sp, QC * c + QC, ALL, crossing, crossed)

            next_indices(0)
            with sp.Fori(1, LAST - 1) as c:
                next_indices(c)
            next_indices(LAST - 1)
            for i in range(CT - 1):
                cross(sp, QC * LAST + QT * (i + 1), tile_w(i), crossing, crossed)
            cross(sp, QC * CHUNKS, tile_w(CT - 1), crossing[SHARE:], crossed)
            sp.wait_ge(y_kept, LAST + CT)
            sp.dma_start(t["y"], yrow[:, :]).then_inc(stored, 16)
            sp.wait_ge(stored, 16)

        @block_.gpsimd
        def _(pool):
            def gather(c, first):
                for i in range(CT):
                    if not first:
                        pool.wait_ge(idx_in[i], 16 * c + 16)
                        pool.wait_ge(transposed, CT * c - (CT - 1 - i))
                        pool.sem_inc(slot_free, 1)
                    else:
                        pool.wait_ge(idx_in[i], 16)
                    for f in [f for f in range(F) if f not in dict(looked(c, i)).values()]:
                        pool.indirect_dma_start(
                            out=emb[:, i, pos(f), :], out_offset=None, in_=t[f"tbl_{f}"],
                            in_offset=bass.IndirectOffsetOnAxis(ap=idx[:, i, f:f + 1], axis=0),
                        ).then_inc(gathered[i], 16)

            gather(0, True)
            with pool.Fori(1, LAST) as c:
                gather(c, False)
            gather(LAST, False)
            cross(pool, QC * CHUNKS, tile_w(CT - 1), crossing[:SHARE], crossed_late)

        @block_.vector
        def _(dve):
            steps = [0]

            def step(ins):
                steps[0] += 1
                ins.then_inc(st_step, 1)

            def settle():
                dve.wait_ge(st_step, steps[0])

            nc.vector.memset(zero[:, :], 0.0).then_inc(ones_set, 1)
            nc.vector.memset(ones[:, :], 1.0).then_inc(ones_set, 1)
            nc.vector.memset(emb[:, :, CONST, :], 1.0).then_inc(ones_set, 1)

            dve.wait_ge(w_in, 32)
            wsame = [w1s[:, k * HH:(k + 1) * HH].rearrange("i (y z) -> i y z", y=FH) for k in range(2)]
            wab = w1s[:, 2 * HH:3 * HH].rearrange("i (y z) -> i y z", y=FH)
            for out, y, z in ((wsame[0], 0, 0), (wsame[1], FH, FH), (wab, 0, FH)):
                step(nc.vector.tensor_tensor(out, w1[:, y:y + FH, z:z + FH],
                                             w1[:, z:z + FH, y:y + FH].rearrange("i z y -> i y z"), ALU.add))
            settle()
            w1flat = w1[:, :, :].rearrange("i y z -> i (y z)")
            for k in range(2):
                first = k * FH * (F + 1)
                step(nc.vector.tensor_copy(w1s[:, k * HH:k * HH + HH:FH + 1],
                                           w1flat[:, first:first + (FH - 1) * (F + 1) + 1:F + 1]))
            nc.vector.tensor_copy(w1s[:, 3 * HH:W1N], b12[:, 0:1]).then_inc(w1_sym, 1)
            step(nc.vector.memset(staging[:, :], 0.0))
            staged["zero"] = steps[0]

            dve.wait_ge(tab_in, 16 * NO + 16)
            step(nc.vector.tensor_copy(parts[:, :, :, 0, :], tab32[:, :, :, :]))
            settle()
            step(nc.vector.tensor_tensor(rest32, tab32, parts[:, :, :, 0, :], ALU.subtract))
            settle()
            step(nc.vector.tensor_copy(parts[:, :, :, 1, :], rest32))
            settle()
            step(nc.vector.tensor_tensor(parts[:, :, :, 2, :], rest32, parts[:, :, :, 1, :], ALU.subtract))
            settle()

            def make_one_hot(c, i):
                n_fields = len(looked(c, i))
                dve.wait_ge(ids_in[i], ids_to(c, i))
                nc.vector.tensor_copy(ids16[:, 0:n_fields, :], ids_all[:, i, 0:n_fields, :]).then_inc(ids_cast, 1)
                dve.wait_ge(ids_cast, c * CT + i + 1)
                for n in range(n_fields):
                    for k in range(OC):
                        last = nc.vector.tensor_scalar(one_hot[:, n, k, :], ids16[:, n, :], row_of[:, k:k + 1], None,
                                                       ALU.is_equal)
                last.then_inc(one_hot_set, 1)

            make_one_hot(0, 0)

            def turn_tile(c, i):
                if looked(c, i):
                    dve.wait_ge(looked_up, c * CT + i + 1)
                    for n, f in looked(c, i):
                        last = nc.vector.tensor_reduce(
                            emb[:, i, pos(f), :], psE[:, n * 3 * K:(n + 1) * 3 * K].rearrange("p (s k) -> p k s", s=3),
                            mybir.AxisListType.X, ALU.add)
                    last.then_inc(summed, 1)
                    dve.wait_ge(summed, c * CT + i + 1)
                dve.wait_ge(gathered[i], gathers_to(c, i))
                nc.vector.transpose(embT[:, i, :, :].rearrange("p a b -> p (a b)"),
                                    emb[:, i, :, :].rearrange("p a b -> p (a b)")).then_inc(transposed, 1)

            def next_one_hot(c, i):
                c1, i1 = (c, i + 1) if i + 1 < CT else (c + 1, 0)
                if looked(c1, i1):
                    make_one_hot(c1, i1)

            def prepare(c, i, hf, only_p=False):
                n = i * 2 + hf
                dve.wait_ge(transposed, c * CT + i + 1)
                if not is_chunk(c, 0):
                    dve.wait_ge(moments, QC * c - QC + QH * (n + 1))
                g0, g1 = hf * HG, hf * HG + HG
                nc.vector.tensor_copy(P[n][:, :, ROW_G:ROW_G + FH + 1],
                                      embT[:, i, 0:FH + 1, g0:g1].rearrange("p f r -> p r f"))
                if not only_p:
                    for q4 in range(Q):
                        nc.vector.tensor_copy(*spread(i, hf, q4))
                for half in range(2):
                    for q in range(FH):
                        lo, hi, s = (pos(x) for x in block(half, q))
                        w = hi - lo + 1
                        r = row(half, q)
                        last = nc.vector.tensor_tensor(
                            P[n][:, :, r:r + w], embT[:, i, lo:hi + 1, g0:g1].rearrange("p f r -> p r f"),
                            embT[:, i, s:s + 1, g0:g1].rearrange("p f r -> p r f").to_broadcast([128, HG, w]),
                            ALU.mult)
                last.then_inc(prepared, 1)

            def tile_of(c, i, last_tile=False):
                turn_tile(c, i)
                for hf in range(2):
                    prepare(c, i, hf)
                if not last_tile:
                    next_one_hot(c, i)

            def two_terms(rules):
                for rule in rules:
                    out, t1, t2, _, _, cols, _, pairs, _, _ = places(*rule)
                    if cols[1] >= cols[0]:
                        step(nc.vector.tensor_tensor(out(*cols, *pairs), t1(*cols, *pairs), t2(*cols, *pairs), ALU.add))

            def add_third(rules):
                for rule in rules:
                    out, _, _, t3, cols, _, _, _, less, _ = places(*rule)
                    if rule[1] > 0:
                        step(nc.vector.tensor_tensor(out(*cols, *less), out(*cols, *less), t3(*cols, *less), ALU.add))

            dve.wait_ge(d_kept, FH)
            two_terms(own_a)
            for rule in a_b:
                out, _, t2, t3, cols, _, _, _, less, _ = places(*rule)
                if rule[1] > 0:
                    step(nc.vector.tensor_tensor(out(*cols, *less), t2(*cols, *less), t3(*cols, *less), ALU.add))
            settle()
            dve.wait_ge(placed, OWN_A)
            add_third(own_a)

            dve.wait_ge(ones_set, 3)
            dve.wait_ge(m_zero, HT)
            turn_tile(0, 0)
            prepare(0, 0, 0, True)

            dve.wait_ge(d_kept, F)
            dve.wait_ge(placed, PA)
            for rule in a_b:
                out, t1, _, _, cols, _, _, pairs, _, _ = places(*rule)
                step(nc.vector.tensor_tensor(out(*cols, *pairs), out(*cols, *pairs), t1(*cols, *pairs), ALU.add))
            two_terms(own_b)
            two_terms(b_a)
            settle()
            dve.wait_ge(placed, PALL)
            add_third(own_b[:LOW_B])
            settle()
            staged["Y"] = steps[0]
            add_third(own_b[LOW_B:])
            add_third(b_a)
            settle()
            staged["X"] = steps[0]
            def weigh(c, w):
                dve.wait_ge(h2_kept, N2 // 128 * c + N2 // 128)
                nc.vector.tensor_scalar(h2w[:, w], h2[:, 0, w], wt3[:, 0:1], None, ALU.mult).then_inc(h2w_set, 1)
                dve.wait_ge(h2w_set, 2 * c + 1)
                nc.vector.scalar_tensor_tensor(out=h2w[:, w], in0=h2[:, 1, w], scalar=wt3[:, 1:2], in1=h2w[:, w],
                                               op0=ALU.mult, op1=ALU.add).then_inc(h2w_set, 1)

            prepare(0, 0, 1, True)
            next_one_hot(0, 0)
            turn_tile(0, 1)
            prepare(0, 1, 0)
            dve.wait_ge(wz_done, len(wz_sets))
            prepare(0, 1, 1)
            next_one_hot(0, 1)
            with dve.Fori(1, LAST) as c:
                for i in range(CT):
                    tile_of(c, i)
                weigh(c - 1, ALL)
            w = ALL
            for i in range(CT):
                tile_of(LAST, i, i == CT - 1)
                weigh(LAST - 1 + i, w)
                w = tile_w(i)
            weigh(LAST + CT - 1, w)

        @block_.tensor
        def _(pe):
            def look_up(c, i):
                pe.wait_ge(one_hot_set, CT * c + i + 1)
                for n, _ in looked(c, i):
                    for k in range(OC):
                        last = nc.tensor.matmul(psE[:, n * 3 * K:(n + 1) * 3 * K], one_hot[:, n, k, :],
                                                parts[:, n, k, :, :].rearrange("p s k -> p (s k)"),
                                                start=(k == 0), stop=(k == OC - 1))
                last.then_inc(looked_up, 1)

            pe.wait_ge(w1_sym, 1)
            for x in range(F):
                if x in W2_CUTS:
                    pe.wait_ge(w2_in[W2_CUTS.index(x)], 16)
                if x >= 4:
                    pe.wait_ge(d_kept, x - 3)
                nc.tensor.matmul(psT[x % 4][:, 0:W1N], w2t[:, x, :], w1s[:, :],
                                 start=True, stop=True).then_inc(d_done, 1)
                if x == F - 6:
                    look_up(0, 0)

            def turn_weights(sets):
                for n in sets:
                    stage, a, _, units, rows, _ = wz_sets[n]
                    pe.wait_ge(st_step, staged["Y" if n < Y_SETS else "X"])
                    pe.wait_ge(placed, PALL + len(places_z))
                    if n >= 2:
                        pe.wait_ge(wz_kept, n - 1)
                    for k in range(units):
                        last = nc.tensor.transpose(psH[n % 2][0:rows, k * H:k * H + H], stage[:, a + k, :], ident[:, :])
                    last.then_inc(wz_done, 1)

            def moments_of(c, quads=range(QC)):
                for k in quads:
                    n, m = k // QH, k % QH
                    i = k // QT
                    if k % QT == QT - (2 if is_chunk(c, 0) or i > 0 else 4) and not is_last_tile(c, i):
                        c1, i1 = (c, i + 1) if i + 1 < CT else (c + 1, 0)
                        if looked(c1, i1):
                            look_up(c1, i1)
                    if m == 0:
                        pe.wait_ge(prepared, 2 * CT * c + n + 1)
                        if is_chunk(c, 0) and n < 2:
                            pe.wait_ge(m_first, Q * (n + 1))
                    again = not (is_chunk(c, 0) and k < 2)
                    if again:
                        pe.wait_ge(x_kept, QC * c + k - 1)
                    for g in range(QUAD):
                        r = m * QUAD + g
                        last = nc.tensor.matmul(psT[2 + k % 2][0:X_ROWS, g * Q * XC:(g + 1) * Q * XC],
                                                P[n][:, r, ROW_X:ROWS], M[:, n, r, :, 0:XC], start=True, stop=True)
                    last.then_inc(x_moments, 1)
                    if again:
                        pe.wait_ge(kept, QC * c + k - 1)
                    for g in range(QUAD):
                        r = m * QUAD + g
                        last = nc.tensor.matmul(psT[k % 2][0:Y_ROWS, g * Q * YC:(g + 1) * Q * YC],
                                                P[n][:, r, 0:Y_ROWS], M[:, n, r, :, LOW_A:NP], start=True, stop=True)
                    last.then_inc(moments, 1)

            z2_units = [(UX + u, rows, TX[0:rows, u, :]) for u in range(FH)
                        for rows in [X_ROWS if 0 < u < LOW_A else 128]]
            z2_units += [(UM + u, 128, TM[:, u, :]) for u in range(NM)]
            z2_units += [(UY + u, Y_ROWS, TY[0:Y_ROWS, u, :]) for u in range(NX)]
            z1_units = [(UZ, 128, TY[:, 0, :]), (UZ + 1, 128, TX[:, CONST, :]), (UZ + 2, 128, TC)]
            z2_half = len(z2_units) // 2


            def z2_first(turn, w, quads):
                pe.wait_ge(kept, quads)
                for n, (unit, rows, rhs) in enumerate(z2_units[:z2_half]):
                    nc.tensor.matmul(psZ[:, CB + w.start:CB + w.stop], wz[0:rows, unit, :], rhs[:, w],
                                     start=(n == 0), stop=False)

            def z2_second(turn, w):
                for n, (unit, rows, rhs) in enumerate(z2_units[z2_half:], z2_half):
                    nc.tensor.matmul(psZ[:, CB + w.start:CB + w.stop], wz[0:rows, unit, :], rhs[:, w],
                                     start=False, stop=(n == len(z2_units) - 1))

            def z1_of(turn, w):
                if is_chunk(turn, LAST + CT - 1):
                    pe.wait_ge(crossed, turn * (16 * len(crossing)) + 16 * len(crossing[SHARE:]))
                    pe.wait_ge(crossed_late, 16 * SHARE)
                else:
                    pe.wait_ge(crossed, (turn + 1) * (16 * len(crossing)))
                for n, (unit, rows, rhs) in enumerate(z1_units):
                    last = nc.tensor.matmul(psZ[:, w], wz[0:rows, unit, :], rhs[:, w],
                                            start=(n == 0), stop=(n == len(z1_units) - 1))
                last.then_inc(z_done, 1)

            def layer1(c, w, b0):
                pe.wait_ge(z_kept, c + 1)
                if not is_chunk(c, 0):
                    pe.wait_ge(h2_kept, N2 // 128 * c)
                    pe.wait_ge(y_kept, c)
                for m in range(N1 // 128):
                    out = psH[m // 2][:, m % 2 * CB + w.start:m % 2 * CB + w.stop]
                    cols = slice(m * 128, m * 128 + 128)
                    nc.tensor.matmul(out, wt1[:, 0, cols], zs[:, 0, w], start=True, stop=False)
                    nc.tensor.matmul(out, wt1[:, 1, cols], zs[:, 1, w], start=False, stop=False)
                    nc.tensor.matmul(out, wt1[0:DC, 2, cols], dense[:, bass.ds(b0, w.stop - w.start)],
                                     start=False, stop=True).then_inc(h1_done, 1)

            def layer2(c, w):
                for m in range(N2 // 128):
                    for k in range(N1 // 128):
                        if m == 0:
                            pe.wait_ge(h1_kept, N1 // 128 * c + max(k + 1, 2))
                        last = nc.tensor.matmul(psH[0][:, m * CB + w.start:m * CB + w.stop],
                                                wt2[:, k, m * 128:m * 128 + 128], h1[:, k, w], start=(k == 0), stop=(k == N1 // 128 - 1))
                    last.then_inc(h2_done, 1)

            def layer3(c, w):
                pe.wait_ge(h2w_set, 2 * c + 2)
                nc.tensor.matmul(psH[1][0:1, w], ones[:, 0:1], h2w[:, w], start=True, stop=True).then_inc(y_done, 1)

            pe.wait_ge(ident_in, 16)
            pe.wait_ge(d_kept, F)
            moments_of(0, range(2))
            turn_weights(range(Y_SETS))
            moments_of(0, range(2, QT))
            turn_weights(range(Y_SETS, len(wz_sets)))
            moments_of(0, range(QT, QC))
            pe.wait_ge(wz_kept, len(wz_sets))
            pe.wait_ge(mlp_in, 6 * 16)
            pe.wait_ge(ones_set, 3)
            z2_first(0, ALL, QC)
            z2_second(0, ALL)
            z1_of(0, ALL)

            def round_(c, before, b0_before):
                moments_of(c, range(QC - QT))
                layer1(before, ALL, b0_before)
                moments_of(c, range(QC - QT, QC))
                layer2(before, ALL)
                z2_first(c, ALL, QC * c + QC)
                layer3(before, ALL)
                z2_second(c, ALL)
                z1_of(c, ALL)

            round_(1, 0, 0)
            with pe.Fori(2, LAST) as c:
                round_(c, c - 1, c * CB - CB)
            before = (LAST - 1, ALL, CB * (LAST - 1))
            for i in range(CT):
                turn, w = LAST + i, tile_w(i)
                if i == 0:
                    moments_of(LAST, range(QT))
                    layer1(*before)
                else:
                    layer1(*before)
                    moments_of(LAST, range(QT * i, QT * i + QT))
                layer2(before[0], before[1])
                z2_first(turn, w, QC * LAST + QT * (i + 1))
                layer3(before[0], before[1])
                z2_second(turn, w)
                z1_of(turn, w)
                before = (turn, w, CB * LAST + i * TILE)
            layer1(*before)
            layer2(before[0], before[1])
            layer3(before[0], before[1])

        @block_.scalar
        def _(act):
            act.dma_start(w1[:, :, :], t["W1"]).then_inc(w_in, 16)
            act.dma_start(b12[:, :], t["b12"]).then_inc(w_in, 16)
            act.wait_ge(ones_set, 1)
            def clear(n):
                nc.scalar.activation(M[:, n, :, :, :].rearrange("p r q j -> p (r q j)"),
                                     zero[:, :].to_broadcast([128, HG * Q * NP]), ACT.Copy).then_inc(m_zero, 1)

            clear(0)
            def place(some):
                for to, from_ in some:
                    nc.scalar.activation(to, from_, ACT.Copy).then_inc(placed, 1)

            for x in range(F):
                act.wait_ge(d_done, x + 1)
                nc.scalar.activation(D[:, x, :], psT[x % 4][:, 0:W1N], ACT.Copy).then_inc(d_kept, 1)
                if x % 3 == 2 and x // 3 + 1 < HT:
                    clear(x // 3 + 1)
                if x == FH:
                    act.wait_ge(d_kept, FH)
                    act.wait_ge(st_step, staged["zero"])
                if x >= FH:
                    place(places_a[(x - FH) * PER_X:(x - FH + 1) * PER_X])
            act.wait_ge(m_zero, HT)
            act.wait_ge(transposed, 1)
            for q4 in range(Q):
                nc.scalar.activation(*spread(0, 0, q4), ACT.Copy).then_inc(m_first, 1)
            act.wait_ge(d_kept, F)
            place(places_all)
            act.wait_ge(w1_sym, 1)
            place(places_z)
            for q4 in range(Q):
                nc.scalar.activation(*spread(0, 1, q4), ACT.Copy).then_inc(m_first, 1)
            def keep_weights(sets):
                for n in sets:
                    _, _, unit, units, rows, p0 = wz_sets[n]
                    act.wait_ge(wz_done, n + 1)
                    nc.scalar.activation(wz[p0:p0 + rows, unit:unit + units, :],
                                         psH[n % 2][0:rows, 0:units * H].rearrange("p (u h) -> p u h", h=H),
                                         ACT.Copy).then_inc(wz_kept, 1)

            def keep_moments(c, tiles=range(CT)):
                for k in range(QT * tiles[0], QT * tiles[-1] + QT):
                    act.wait_ge(x_moments, QC * c + k + 1)
                    b = slice(k * QUAD * Q, (k + 1) * QUAD * Q)
                    Y, X = (ps[:, 0:QUAD * Q * n].rearrange("p (x j) -> p j x", j=n)
                            for ps, n in ((psT[k % 2], YC), (psT[2 + k % 2], XC)))
                    nc.scalar.activation(TX[0:X_ROWS, :, b], X[0:X_ROWS, 0:NX, :], ACT.Copy)
                    for p, cols in ((0, M_LOW), (CORNER, NM)):
                        nc.scalar.activation(TM[p + CORNER:p + 2 * CORNER, 0:cols, b],
                                             X[p:p + CORNER, NX:NX + cols, :], ACT.Copy)
                    corners = T[X_ROWS:128, 0:2 * FH, b].rearrange("p (k u) b -> p k u b", k=2)
                    nc.scalar.activation(corners[:, :, 0:NM, :],
                                         X[X_ROWS - CORNER:X_ROWS, NX:XC, :].rearrange("p (k u) b -> p k u b", k=2),
                                         ACT.Copy).then_inc(x_kept, 1)
                    act.wait_ge(moments, QC * c + k + 1)
                    nc.scalar.activation(TY[0:Y_ROWS, :, b], Y[0:Y_ROWS, YC - NX:YC, :], ACT.Copy)
                    nc.scalar.activation(TX[X_ROWS:128, LOW_A:A1, b], Y[0:CORNER, 0:NA, :], ACT.Copy)
                    nc.scalar.activation(TX[X_ROWS:128, 0:1, b], Y[CORNER:2 * CORNER, NA - 1:NA, :], ACT.Copy)
                    act.wait_ge(x_kept, QC * c + k + 1)
                    for m, rows in enumerate(A_ROWS):
                        last = nc.scalar.activation(TM[0:rows, m:m + 1, b], Y[0:rows, NA + m:NA + m + 1, :], ACT.Copy)
                    last.then_inc(kept, 1)

            def keep_z(c, w):
                act.wait_ge(z_done, c + 1)
                nc.scalar.activation(zs[:, :, w], psZ[:, :].rearrange("p (z b) -> p z b", z=2)[:, :, w],
                                     ACT.Copy).then_inc(z_kept, 1)

            def keep_h1(c, w):
                for m in range(N1 // 128):
                    act.wait_ge(h1_done, N1 // 128 * c + m // 2 * 2 + 2)
                    nc.scalar.activation(h1[:, m, w], psH[m // 2][:, m % 2 * CB + w.start:m % 2 * CB + w.stop], ACT.Relu,
                                         bias=bt[:, m:m + 1]).then_inc(h1_kept, 1)

            def keep_h2(c, w):
                act.wait_ge(h2_done, N2 // 128 * c + N2 // 128)
                for m in range(N2 // 128):
                    nc.scalar.activation(h2[:, m, w], psH[0][:, m * CB + w.start:m * CB + w.stop], ACT.Relu,
                                         bias=bt[:, N1 // 128 + m:N1 // 128 + m + 1]).then_inc(h2_kept, 1)

            def keep_y(c, w, b0):
                act.wait_ge(y_done, c + 1)
                nc.scalar.activation(
                    yrow[:, bass.ds(b0, w.stop - w.start)].rearrange("o (t q r) -> o t r q", q=Q, r=GR),
                    psH[1][0:1, w].rearrange("o (t r q) -> o t r q", q=Q, r=GR), ACT.Copy).then_inc(y_kept, 1)

            keep_weights(range(Y_SETS))
            act.wait_ge(st_step, staged["X"])
            keep_moments(0, range(1))
            keep_weights(range(Y_SETS, len(wz_sets)))
            keep_moments(0, range(1, CT))
            act.wait_ge(mlp_in, 6 * 16)
            keep_z(0, ALL)
            with act.Fori(1, LAST) as c:
                keep_moments(c, range(CT - 1))
                keep_h1(c - 1, ALL)
                keep_moments(c, range(CT - 1, CT))
                keep_h2(c - 1, ALL)
                keep_y(c - 1, ALL, c * CB - CB)
                keep_z(c, ALL)
            before = (LAST - 1, ALL, CB * (LAST - 1))
            for i in range(CT):
                if i == 0:
                    keep_moments(LAST, range(1))
                    keep_h1(before[0], before[1])
                else:
                    keep_h1(before[0], before[1])
                    keep_moments(LAST, range(i, i + 1))
                keep_h2(before[0], before[1])
                keep_y(*before)
                keep_z(LAST + i, tile_w(i))
                before = (LAST + i, tile_w(i), CB * LAST + i * TILE)
            keep_h1(before[0], before[1])
            keep_h2(before[0], before[1])
            keep_y(*before)


def kernel(**inputs):
    import numpy as np
    import concourse.bacc as bacc
    from concourse.bass_utils import run_bass_kernel_spmd

    B, F = inputs["ids"].shape
    K = inputs["tbl_0"].shape[1]
    Q, GR = 128 // K, 128 // (128 // K)
    a = {f"tbl_{f}": inputs[f"tbl_{f}"] for f in range(F)}
    a["ids"] = inputs["ids"]
    a["denseT"] = inputs["dense_ctx"].reshape(B // 128, Q, GR, -1).transpose(3, 0, 2, 1).reshape(-1, B)
    a["idsT"] = inputs["ids"].T
    a["row_of"] = np.arange(1000, dtype=np.float32).reshape(-1, 8)
    a["W1"] = inputs["L0_rec_W1"]
    a["W2t"] = inputs["L0_rec_W2"].transpose(1, 2, 0)
    a["b12"] = np.stack([inputs["L0_rec_b1"], inputs["L0_rec_b2"]], axis=1)
    a["W_top1"] = inputs["W_top1"]
    a["W_top2"] = inputs["W_top2"]
    a["W_top3p"] = inputs["W_top3"].reshape(-1, 128).T
    a["b_top"] = np.concatenate([inputs["b_top1"].reshape(-1, 128), inputs["b_top2"].reshape(-1, 128)]).T
    a["ident"] = np.eye(128, dtype=np.float32)
    a = {k: np.ascontiguousarray(v) for k, v in a.items()}

    nc = bacc.Bacc("TRN2", target_bir_lowering=False, num_devices=1)
    t = {k: nc.dram_tensor(f"in_{k}", v.shape, mybir.dt.from_np(v.dtype), kind="ExternalInput").ap()
         for k, v in a.items()}
    t["y"] = nc.dram_tensor("out_y", (1, B), F32, kind="ExternalOutput").ap()
    build_dlrm_tower(nc, t)
    r = run_bass_kernel_spmd(nc, [{f"in_{k}": v for k, v in a.items()}], core_ids=[0])
    return r.results[0]["out_y"].reshape(B, 1)
```
